# Optimizing a Trainium2 kernel written in Bass

```python
import numpy as np
import jax
import jax.numpy as jnp

def _softmax(x, axis=-1):
    return jax.nn.softmax(x, axis=axis)

def _gelu(x):
    return jax.nn.gelu(x, approximate=True)

def _silu(x):
    return jax.nn.silu(x)

def _sigmoid(x):
    return jax.nn.sigmoid(x)

def _layernorm(x, axis=-1, eps=1e-05):
    m = jnp.mean(x, axis=axis, keepdims=True)
    v = jnp.var(x, axis=axis, keepdims=True)
    return (x - m) / jnp.sqrt(v + eps)

def _scatter_add(tgt, idx, src, axis=0):
    return tgt.at[idx].add(src)

def _segment_sum(src, seg, n):
    return jax.ops.segment_sum(src, seg, n)
kernel_name = 'mk_prb_d1_jaxref_r8_44defb'

def setup_inputs(seed: int=0):
    np.random.seed(seed)
    _w = jnp.asarray

    def _L0_attn_setup():
        import jax, jax.numpy as jnp
        import numpy as np
        DT_MIN, DT_MAX = (0.001, 0.1)
        EPS = 1e-05

        def rmsnorm(x, w):
            return x * jax.lax.rsqrt(jnp.mean(x * x, axis=-1, keepdims=True) + EPS) * w
        key = jax.random.key(seed)
        ks = jax.random.split(key, 12)
        B, T, D = (1, 256, 128)
        E, N, I, K = (2 * D, 64, 256, 4)
        s = lambda k, sh, fan: jax.random.normal(k, sh, jnp.float32) / np.sqrt(fan).astype(np.float32)
        return {'x': jax.random.normal(ks[0], (B, T, D), jnp.float32), 'input_norm_w': jnp.ones((D,), jnp.float32), 'ffn_norm_w': jnp.ones((D,), jnp.float32), 'in_proj_W': s(ks[1], (D, 2 * E), D), 'conv_W': s(ks[2], (K, 1, E), K), 'conv_b': jnp.zeros((E,), jnp.float32), 'dt_W': s(ks[3], (E, E), E), 'dt_b': jnp.zeros((E,), jnp.float32), 'B_W': s(ks[4], (E, N), E), 'C_W': s(ks[5], (E, N), E), 'A_log': -jnp.log(jnp.arange(1, N + 1, dtype=jnp.float32)), 'out_proj_W': s(ks[6], (E, D), E), 'gate_W': s(ks[7], (D, I), D), 'up_W': s(ks[8], (D, I), D), 'down_W': s(ks[9], (I, D), I)}
    _L0_attn_in = _L0_attn_setup()

    def _L0_ffn_setup():
        import jax, jax.numpy as jnp
        import numpy as np
        import math
        D_IN = 128
        FEATURES = (512, 512, 128)
        BATCH, SEQ = (8, 256)

        def _conn_dense(kernel_bool, x):
            w = jnp.where(kernel_bool, jnp.float32(1.0), jnp.float32(-1.0))
            return x @ w
        key = jax.random.key(seed)
        kx, kk0, kk1, kk2 = jax.random.split(key, 4)
        x = jax.random.normal(kx, (BATCH, SEQ, D_IN), dtype=jnp.float32)
        k0 = jax.random.randint(kk0, (2 * D_IN, FEATURES[0]), 0, 2).astype(jnp.bool_)
        k1 = jax.random.randint(kk1, (FEATURES[0], FEATURES[1]), 0, 2).astype(jnp.bool_)
        k2 = jax.random.randint(kk2, (FEATURES[1], FEATURES[2]), 0, 2).astype(jnp.bool_)
        s0 = jnp.asarray(1.0 / math.sqrt(2 * D_IN), dtype=jnp.float32)
        s1 = jnp.asarray(1.0 / math.sqrt(FEATURES[0]), dtype=jnp.float32)
        s2 = jnp.asarray(1.0 / math.sqrt(FEATURES[1]), dtype=jnp.float32)
        return {'x': x, 'k0': k0, 'k1': k1, 'k2': k2, 's0': s0, 's1': s1, 's2': s2}
    _L0_ffn_in = _L0_ffn_setup()
    _d = {'L0_attn_x': _L0_attn_in['x'], 'L0_attn_input_norm_w': _L0_attn_in['input_norm_w'], 'L0_attn_ffn_norm_w': _L0_attn_in['ffn_norm_w'], 'L0_attn_in_proj_W': _L0_attn_in['in_proj_W'], 'L0_attn_conv_W': _L0_attn_in['conv_W'], 'L0_attn_conv_b': _L0_attn_in['conv_b'], 'L0_attn_dt_W': _L0_attn_in['dt_W'], 'L0_attn_dt_b': _L0_attn_in['dt_b'], 'L0_attn_B_W': _L0_attn_in['B_W'], 'L0_attn_C_W': _L0_attn_in['C_W'], 'L0_attn_A_log': _L0_attn_in['A_log'], 'L0_attn_out_proj_W': _L0_attn_in['out_proj_W'], 'L0_attn_gate_W': _L0_attn_in['gate_W'], 'L0_attn_up_W': _L0_attn_in['up_W'], 'L0_attn_down_W': _L0_attn_in['down_W'], 'L0_ffn_k0': _L0_ffn_in['k0'], 'L0_ffn_k1': _L0_ffn_in['k1'], 'L0_ffn_k2': _L0_ffn_in['k2'], 'L0_ffn_s0': _L0_ffn_in['s0'], 'L0_ffn_s1': _L0_ffn_in['s1'], 'L0_ffn_s2': _L0_ffn_in['s2']}
    _x0 = _d['L0_attn_x']
    _d['L0_attn_x'] = jax.random.normal(jax.random.fold_in(jax.random.key(seed), 1), (8, 512, 128), dtype=_x0.dtype)
    del _x0
    return _d

def reference(L0_attn_x, L0_attn_input_norm_w, L0_attn_ffn_norm_w, L0_attn_in_proj_W, L0_attn_conv_W, L0_attn_conv_b, L0_attn_dt_W, L0_attn_dt_b, L0_attn_B_W, L0_attn_C_W, L0_attn_A_log, L0_attn_out_proj_W, L0_attn_gate_W, L0_attn_up_W, L0_attn_down_W, L0_ffn_k0, L0_ffn_k1, L0_ffn_k2, L0_ffn_s0, L0_ffn_s1, L0_ffn_s2):

    def _L0_attn_ref(x, input_norm_w, ffn_norm_w, in_proj_W, conv_W, conv_b, dt_W, dt_b, B_W, C_W, A_log, out_proj_W, gate_W, up_W, down_W):
        import jax, jax.numpy as jnp
        import numpy as np
        DT_MIN, DT_MAX = (0.001, 0.1)
        EPS = 1e-05

        def rmsnorm(x, w):
            return x * jax.lax.rsqrt(jnp.mean(x * x, axis=-1, keepdims=True) + EPS) * w
        Bsz, T, D = x.shape
        E = in_proj_W.shape[1] // 2
        N = A_log.shape[0]
        normed = rmsnorm(x, input_norm_w)
        xp = normed @ in_proj_W
        x_z, z = (xp[..., :E], xp[..., E:])
        xc = jax.lax.conv_general_dilated(x_z, conv_W, window_strides=(1,), padding='SAME', dimension_numbers=('NWC', 'WIO', 'NWC'), feature_group_count=E) + conv_b
        xc = jax.nn.silu(xc)
        dt = jnp.clip(jax.nn.softplus(xc @ dt_W + dt_b), DT_MIN, DT_MAX)
        Bp = xc @ B_W
        Cp = xc @ C_W
        A = -jnp.exp(A_log)

        def step(h, ins):
            x_t, dt_t, B_t, C_t = ins
            dA = jnp.exp(dt_t[..., None] * A)
            h = dA * h + dt_t[..., None] * B_t[:, None, :] * x_t[..., None]
            y_t = jnp.einsum('ben,bn->be', h, C_t)
            return (h, y_t)
        h0 = jnp.zeros((Bsz, E, N), x.dtype)
        _, y = jax.lax.scan(step, h0, (xc.transpose(1, 0, 2), dt.transpose(1, 0, 2), Bp.transpose(1, 0, 2), Cp.transpose(1, 0, 2)))
        y = y.transpose(1, 0, 2) * jax.nn.silu(z)
        x = x + y @ out_proj_W
        n2 = rmsnorm(x, ffn_norm_w)
        ffn = jax.nn.silu(n2 @ gate_W) * (n2 @ up_W) @ down_W
        return x + ffn

    def _L0_ffn_ref(x, k0, k1, k2, s0, s1, s2):
        import jax, jax.numpy as jnp
        import numpy as np
        import math
        D_IN = 128
        FEATURES = (512, 512, 128)
        BATCH, SEQ = (8, 256)

        def _conn_dense(kernel_bool, x):
            w = jnp.where(kernel_bool, jnp.float32(1.0), jnp.float32(-1.0))
            return x @ w
        h = jnp.concatenate([x, -x], axis=-1)
        h = s0 * _conn_dense(k0, h)
        h = jax.nn.relu(h) * 2
        h = s1 * _conn_dense(k1, h)
        h = jax.nn.relu(h) * 2
        h = s2 * _conn_dense(k2, h)
        return h
    x = L0_attn_x
    xn = _layernorm(x, axis=-1)
    x = x + _L0_attn_ref(xn, L0_attn_input_norm_w, L0_attn_ffn_norm_w, L0_attn_in_proj_W, L0_attn_conv_W, L0_attn_conv_b, L0_attn_dt_W, L0_attn_dt_b, L0_attn_B_W, L0_attn_C_W, L0_attn_A_log, L0_attn_out_proj_W, L0_attn_gate_W, L0_attn_up_W, L0_attn_down_W) + _L0_ffn_ref(xn, L0_ffn_k0, L0_ffn_k1, L0_ffn_k2, L0_ffn_s0, L0_ffn_s1, L0_ffn_s2)
    return x

_drawn_inputs = setup_inputs


def setup_inputs(seed=0):
    import zlib

    import numpy as np

    out = dict(_drawn_inputs(seed))
    spreads = {'L0_attn_input_norm_w': (1.0, 0.2),
     'L0_attn_ffn_norm_w': (1.0, 0.2),
     'L0_attn_conv_b': (0.0, 0.1),
     'L0_attn_dt_b': (0.0, 0.8)}
    factors = {'L0_attn_dt_W': 8.0}
    for name, (base, spread) in spreads.items():
        noise = np.random.default_rng([zlib.crc32(name.encode()), seed]).standard_normal(out[name].shape)
        drawn = base * np.exp(spread * noise) if base else spread * noise
        out[name] = jnp.asarray(drawn.astype(out[name].dtype))
    for name, factor in factors.items():
        out[name] = (out[name] * factor).astype(out[name].dtype)
    return out
```

```python
from contextlib import ExitStack

import concourse.bass as bass
from concourse import mybir

F32 = mybir.dt.float32
BF16 = mybir.dt.bfloat16
U8 = mybir.dt.uint8
ALU = mybir.AluOpType
ACT = mybir.ActivationFunctionType

P = 128
EPS = 1e-5
DT_MIN, DT_MAX = 0.001, 0.1


def mamba_and_binary_mlp_block(nc: bass.Bass, x, norm_w, ffn_w, in_w, conv_w, conv_b, dt_w, dt_b, b_w, c_w,
                               a_log, out_w, gate_w, up_w, down_w, k0, k1, k2, s0, s1, s2, out):
    B, T, D = x.shape
    E = in_w.shape[1] // 2
    N = a_log.shape[0]
    I = gate_w.shape[1]
    H1, H2 = k0.shape[1], k1.shape[1]
    EH = E // P
    IH = I // P
    NJ = T // P
    NP = 3
    Q = B // 2
    TAPS = conv_w.shape[0]
    PAD_L = (TAPS - 1) // 2
    TPAD = T + TAPS - 1
    assert D == P and 2 * N == P and T % P == 0

    TC = 16
    NC = T // TC
    UROWS = NP * NP * B
    KROWS = UROWS + NP * B
    QE = Q * E
    SELF = QE // 2
    RING = 4
    STEPS = 2 * TC
    LAG = 2

    TG = 64
    NG = T // TG
    GT = TG // TC
    GTOK = GT * P

    u_stage = nc.dram_tensor("u_stage", (NP, B, T, E), BF16, kind="Internal").ap()
    dt_stage = nc.dram_tensor("dt_stage", (NP, B, T, E), BF16, kind="Internal").ap()
    b_stage = nc.dram_tensor("b_stage", (NP, NP, B, T, N), BF16, kind="Internal").ap()

    with ExitStack() as ctx:
        def sb(name, shape, dt=F32):
            return ctx.enter_context(nc.sbuf_tensor(name, shape, dt))

        def sem(name):
            return ctx.enter_context(nc.semaphore(name))

        ps = ctx.enter_context(nc.psum_tensor("ps", [P, 8, 512], F32))

        ident = sb("ident", [P, P])
        zero_w = sb("zero_w", [P, P])
        mhalf = sb("mhalf", [P, NJ])
        w_in = sb("w_in", [P, 2 * E])
        conv_bc = sb("conv_bc", [P, TAPS, E])
        w_tap = sb("w_tap", [P, TAPS, E])
        w_dtb = sb("w_dtb", [P, EH, E + N])
        w_c = sb("w_c", [P, EH, N])
        w_out = sb("w_out", [P, EH, D])
        w_gate = sb("w_gate", [P, I])
        w_up = sb("w_up", [P, I])
        w_down = sb("w_down", [P, IH, D])
        nw_col = sb("nw_col", [P, 1])
        fw_col = sb("fw_col", [P, 1])
        cb_col = sb("cb_col", [P, EH])
        dtb_bc = sb("dtb_bc", [P, E])
        a_col = sb("a_col", [P, 3])
        s_col = sb("s_col", [P, 3])
        s_fold = sb("s_fold", [P, 2])
        w0 = sb("w0", [P, H1])
        w1 = sb("w1", [P, H1 // P, H2])
        w2 = sb("w2", [P, H2 // P, D])

        silu_z = sb("silu_z", [P, EH, B, T])
        c_feat = sb("c_feat", [P, Q, T])
        y_all = sb("y_all", [P, NC, E])

        wait_mark = sb("wait_mark", [P, 1])
        inv_d = sb("inv_d", [P, NJ])
        eps_t = sb("eps_t", [P, NJ])
        weights = sem("weights")
        const_zero = sem("const_zero")
        const_done = sem("const_done")
        taps_ready = sem("taps_ready")
        bin_raw = sem("bin_raw")
        bin_ready = sem("bin_ready")
        a_exp = sem("a_exp")
        a_ready = sem("a_ready")

        def settle(eng):
            eng.wait_ge(weights, NWEIGHTS)

        def wait_all(eng, waits):
            settle(eng)
            for s, v in waits:
                if not (isinstance(v, int) and v <= 0):
                    eng.wait_ge(s, v)

        with ExitStack() as c0:
            k0_raw = c0.enter_context(nc.sbuf_tensor("k0_raw", [P, 2, H1], U8))
            k1_raw = c0.enter_context(nc.sbuf_tensor("k1_raw", [P, H1 // P, H2], U8))
            k2_raw = c0.enter_context(nc.sbuf_tensor("k2_raw", [P, H2 // P, D], U8))
            k0_f = c0.enter_context(nc.sbuf_tensor("k0_f", [P, H1], F32))
            with nc.Block() as block:
                loads = [
                    (w_in[:], in_w), (w_dtb[:, :, 0:E], dt_w.rearrange("(h p) e -> p h e", p=P)),
                    (w_dtb[:, :, E:E + N], b_w.rearrange("(h p) n -> p h n", p=P)),
                    (w_c[:], c_w.rearrange("(h p) n -> p h n", p=P)),
                    (w_out[:], out_w.rearrange("(h p) d -> p h d", p=P)),
                    (w_gate[:], gate_w), (w_up[:], up_w), (w_down[:], down_w.rearrange("(h p) d -> p h d", p=P)),
                    (k0_raw[:], k0.rearrange("(h p) f -> p h f", p=P)),
                    (k1_raw[:], k1.rearrange("(h p) f -> p h f", p=P)),
                    (k2_raw[:], k2.rearrange("(h p) f -> p h f", p=P)),
                    (conv_bc[:], conv_w.rearrange("k o e -> o k e").partition_broadcast(P).rearrange("p o k e -> p (o k) e")),
                    (dtb_bc[:], dt_b.partition_broadcast(P)),
                    (nw_col[:], norm_w.unsqueeze(1)), (fw_col[:], ffn_w.unsqueeze(1)),
                    (a_col[0:N, 0:1], a_log.unsqueeze(1)), (a_col[N:P, 0:1], a_log.unsqueeze(1)),
                    (s_col[:, 0:1], s0.partition_broadcast(P)), (s_col[:, 1:2], s1.partition_broadcast(P)),
                    (s_col[:, 2:3], s2.partition_broadcast(P)),
                ] + [(cb_col[:, h:h + 1], conv_b[h * P:(h + 1) * P].unsqueeze(1)) for h in range(EH)]
                NWEIGHTS = 16 * len(loads)

                @block.sync
                def _(sp):
                    for dst, src in loads:
                        sp.dma_start(dst, src, allow_slow_non_contiguous=True).then_inc(weights, 16)
                    sp.wait_ge(weights, NWEIGHTS)

                @block.gpsimd
                def _(pool):
                    nc.gpsimd.memset(ident[:], 0.0).then_inc(const_zero, 1)
                    nc.gpsimd.memset(zero_w[:], 0.0)
                    nc.gpsimd.memset(mhalf[:], -0.5)
                    nc.gpsimd.memset(eps_t[:], EPS)
                    nc.gpsimd.memset(inv_d[:], 1.0 / D)
                    pool.wait_ge(const_zero, 1)
                    nc.gpsimd.affine_select(out=ident[:], in_=ident[:], compare_op=ALU.not_equal, fill=1.0, base=0,
                                            pattern=[[-1, P]], channel_multiplier=1).then_inc(const_done, 1)

                @block.scalar
                def _(act):
                    act.wait_ge(weights, NWEIGHTS)
                    nc.scalar.activation(a_col[:, 1:2], a_col[:, 0:1], ACT.Exp).then_inc(a_exp, 1)
                    act.wait_ge(a_exp, 1)
                    nc.scalar.mul(a_col[:, 2:3], a_col[:, 1:2], -1.0).then_inc(a_ready, 1)

                @block.vector
                def _(dve):
                    dve.wait_ge(weights, NWEIGHTS)
                    for k in range(TAPS):
                        tap = nc.vector.tensor_tensor(w_tap[:, k, :], w_in[:, 0:E], conv_bc[:, k, :], ALU.mult)
                    tap.then_inc(taps_ready, 1)
                    nc.vector.tensor_copy(k0_f[:], k0_raw[:, 1, :]).then_inc(bin_raw, 1)
                    nc.vector.tensor_scalar(s_fold[:], s_col[:, 1:3], 2.0, None, ALU.mult).then_inc(bin_raw, 1)
                    nc.vector.tensor_scalar(w1[:], k1_raw[:], 2.0, -1.0, ALU.mult, ALU.add)
                    nc.vector.tensor_scalar(w2[:], k2_raw[:], 2.0, -1.0, ALU.mult, ALU.add).then_inc(bin_raw, 1)
                    dve.wait_ge(bin_raw, 3)
                    nc.vector.tensor_tensor(w0[:], k0_raw[:, 0, :], k0_f[:], ALU.subtract).then_inc(bin_raw, 1)
                    nc.vector.tensor_scalar(w2[:], w2[:], s_fold[:, 1:2], None, ALU.mult).then_inc(bin_ready, 1)
                    dve.wait_ge(bin_raw, 4)
                    nc.vector.tensor_scalar(w0[:], w0[:], 2.0, None, ALU.mult).then_inc(bin_ready, 1)

        with ExitStack() as c1:
            def pb(name, shape, dt=F32):
                return c1.enter_context(nc.sbuf_tensor(name, shape, dt))

            x_tok = pb("x_tok", [P, 2, NJ, D])
            stats = pb("stats", [P, 2, NJ, 6])
            mean_var = pb("mean_var", [P, 2, NJ, 2])
            nrm = pb("nrm", [P, 6, NJ])
            normed = pb("normed", [P, 2, NJ, D])
            n_feat = pb("n_feat", [P, 2, TPAD])
            xc_feat = pb("xc_feat", [P, 2, EH, T])
            soft = pb("soft", [P, 4, NJ, E])
            dt_tok = pb("dt_tok", [P, NJ, E])
            u_tok = pb("u_tok", [P, NJ, E])
            b_tok = pb("b_tok", [P, NJ, N])
            dt_rest = pb("dt_rest", [P, NJ, E])
            u_rest = pb("u_rest", [P, NJ, E])
            b_rest = pb("b_rest", [P, NJ, N])
            dt_parts = pb("dt_parts", [P, NP, NJ, E], BF16)
            u_parts = pb("u_parts", [P, NP, NJ, E], BF16)
            b_parts = pb("b_parts", [P, NP, NJ, N], BF16)

            names = ("x_loaded0 x_loaded1 stats_ready moments_ready rms_ready normed_ready normed_t_ready n_feat_ready "
                     "xc_proj_ready z_proj_ready xc_ready z_ready tok_proj_ready xc_t_ready c_proj_ready c_ready "
                     "v_ready exp_ready p_ready ln_ready log_err_ready dt0_ready dt_ready u_ready "
                     "b_copied dt_split u_split b_split parts_stored pads_ready nrm_step split_step "
                     "dt_hi_ready u_hi_ready b_hi_ready dt_r1_ready u_r1_ready b_r1_ready dt_mid_ready u_mid_ready b_mid_ready w1_step")
            S = {n: sem(n) for n in names.split()}

            def batches(eng, body):
                for bb in range(2):
                    body(0, bb)
                with eng.Fori(1, Q) as q:
                    for bb in range(2):
                        body(q, bb)

            def after(eng, name, n, per=1, back=0):
                if isinstance(n, int) and n - back < 0:
                    return
                eng.wait_ge(S[name], (n - back + 1) * per)

            NRM, XC, CB, ZB, TOK = 0, 1, 3, 4, 4

            with nc.Block() as block:
                @block.sync
                def _(sp):
                    def load(q, bb):
                        n = q * 2 + bb
                        wait_all(sp, [(S["normed_ready"], n - 1)])
                        sp.dma_start(x_tok[:, bb], x[bass.ds(n, 1)].rearrange("o (p j) d -> (o p) j d", j=NJ)
                                     ).then_inc(S[f"x_loaded{bb}"], 16)

                    def store(q, bb):
                        n = q * 2 + bb
                        for parts, stage, split in ((dt_parts, dt_stage, "dt_split"), (u_parts, u_stage, "u_split")):
                            wait_all(sp, [(S[split], n + 1)])
                            for i in range(NP):
                                sp.dma_start(stage[i, bass.ds(n, 1)].rearrange("o (p j) e -> (o p) (j e)", j=NJ),
                                             parts[:, i].rearrange("p j e -> p (j e)")).then_inc(S["parts_stored"], 16)
                        wait_all(sp, [(S["b_split"], n + 1)])
                        for j in range(NP):
                            for i in range(NP):
                                sp.dma_start(b_stage[j, i, bass.ds(n, 1)].rearrange("o (p j) e -> (o p) (j e)", j=NJ),
                                             b_parts[:, j].rearrange("p j e -> p (j e)")).then_inc(S["parts_stored"], 16)

                    load(0, 0)
                    load(0, 1)
                    store(0, 0)
                    load(1, 0)
                    store(0, 1)
                    load(1, 1)
                    with sp.Fori(1, Q - 1) as q:
                        for bb in range(2):
                            store(q, bb)
                            load(q + 1, bb)
                    for bb in range(2):
                        store(Q - 1, bb)
                    sp.wait_ge(S["parts_stored"], 16 * B * (2 * NP + NP * NP))

                @block.gpsimd
                def _(pool):
                    nc.gpsimd.memset(n_feat[:, :, 0:PAD_L], 0.0)
                    nc.gpsimd.memset(n_feat[:, :, PAD_L + T:TPAD], 0.0).then_inc(S["pads_ready"], 1)

                    def body(q, bb):
                        n = q * 2 + bb
                        after(pool, "moments_ready", n)
                        after(pool, "normed_ready", n, back=1)
                        var = mean_var[:, bb, :, 1]
                        steps = [
                            lambda: nc.gpsimd.tensor_tensor(nrm[:, 0], var, eps_t[:], ALU.add),
                            lambda: nc.gpsimd.tensor_tensor(nrm[:, 1], nrm[:, 0], mhalf[:], ALU.pow),
                            lambda: nc.gpsimd.tensor_tensor(nrm[:, 2], var, nrm[:, 1], ALU.mult),
                            lambda: nc.gpsimd.tensor_tensor(nrm[:, 3], nrm[:, 2], nrm[:, 1], ALU.mult),
                            lambda: nc.gpsimd.tensor_tensor(nrm[:, 3], nrm[:, 3], eps_t[:], ALU.add),
                            lambda: nc.gpsimd.tensor_tensor(nrm[:, 4], nrm[:, 3], mhalf[:], ALU.pow),
                        ]
                        for k, step in enumerate(steps):
                            step().then_inc(S["nrm_step"], 1)
                            pool.wait_ge(S["nrm_step"], n * len(steps) + k + 1)
                        nc.gpsimd.tensor_tensor(nrm[:, 5], nrm[:, 4], nrm[:, 1], ALU.mult).then_inc(S["rms_ready"], 1)
                        after(pool, "p_ready", n)
                        after(pool, "dt0_ready", n, back=1)
                        nc.gpsimd.tensor_tensor(soft[:, 3], soft[:, 2], soft[:, 1], ALU.subtract
                                                ).then_inc(S["log_err_ready"], 1)
                        after(pool, "dt_hi_ready", n)
                        nc.gpsimd.tensor_tensor(dt_rest[:], dt_tok[:], dt_parts[:, 0], ALU.subtract
                                                ).then_inc(S["dt_r1_ready"], 1)
                        after(pool, "dt_mid_ready", n)
                        nc.gpsimd.tensor_tensor(dt_parts[:, 2], dt_rest[:], dt_parts[:, 1], ALU.subtract
                                                ).then_inc(S["dt_split"], 1)

                    batches(pool, body)

                @block.tensor
                def _(pe):
                    pe.wait_ge(const_done, 1)
                    pe.wait_ge(taps_ready, 1)

                    def body(q, bb):
                        n = q * 2 + bb
                        after(pe, "normed_ready", n)
                        after(pe, "n_feat_ready", n, back=1)
                        for j in range(NJ):
                            m = nc.tensor.transpose(ps[:, NRM, j * P:(j + 1) * P], normed[:, bb, j], ident[:])
                        m.then_inc(S["normed_t_ready"], 1)
                        after(pe, "n_feat_ready", n)
                        after(pe, "u_ready", n, back=1)
                        for h in range(EH):
                            for k in range(TAPS):
                                m = nc.tensor.matmul(ps[:, XC + h, :], w_tap[:, k, h * P:(h + 1) * P],
                                                     n_feat[:, bb, k:k + T], start=(k == 0), stop=(k == TAPS - 1))
                        m.then_inc(S["xc_proj_ready"], 1)
                        after(pe, "v_ready", n, back=1)
                        after(pe, "b_copied", n, back=1)
                        for h in range(EH):
                            m = nc.tensor.matmul(ps[:, ZB + h, :], w_in[:, E + h * P:E + (h + 1) * P],
                                                 n_feat[:, bb, PAD_L:PAD_L + T], start=True, stop=True)
                        m.then_inc(S["z_proj_ready"], 1)
                        after(pe, "xc_ready", n)
                        after(pe, "c_ready", n, back=1)
                        for h in range(EH):
                            m = nc.tensor.matmul(ps[bb * N:(bb + 1) * N, CB, :], w_c[:, h, :], xc_feat[:, bb, h, :],
                                                 start=(h == 0), stop=(h == EH - 1))
                        m.then_inc(S["c_proj_ready"], 1)
                        for j in range(NJ):
                            for h in range(EH):
                                m = nc.tensor.transpose(
                                    ps[:, XC + j // 2, (j % 2) * E + h * P:(j % 2) * E + (h + 1) * P],
                                    xc_feat[:, bb, h, j:T:NJ], ident[:])
                        m.then_inc(S["xc_t_ready"], 1)
                        after(pe, "z_ready", n)
                        for j in range(NJ):
                            for h in range(EH):
                                m = nc.tensor.matmul(ps[:, TOK + j, 0:E + N], xc_feat[:, bb, h, j:T:NJ], w_dtb[:, h, :],
                                                     start=(h == 0), stop=(h == EH - 1))
                        m.then_inc(S["tok_proj_ready"], 1)

                    batches(pe, body)

                @block.scalar
                def _(act):
                    act.wait_ge(weights, NWEIGHTS)
                    act.wait_ge(S["pads_ready"], 1)

                    def body(q, bb):
                        n = q * 2 + bb
                        after(act, "normed_t_ready", n)
                        after(act, "z_proj_ready", n, back=2)
                        nc.scalar.activation(
                            n_feat[:, bb, PAD_L:PAD_L + T].rearrange("d (p j) -> d p j", j=NJ),
                            ps[:, NRM, :].rearrange("d (j p) -> d p j", j=NJ), ACT.Copy, scale=nw_col[:, 0:1]
                        ).then_inc(S["n_feat_ready"], 1)
                        after(act, "xc_proj_ready", n)
                        after(act, "tok_proj_ready", n, back=2)
                        for h in range(EH):
                            m = nc.scalar.activation(xc_feat[:, bb, h, :], ps[:, XC + h, :], ACT.Silu,
                                                     bias=cb_col[:, h:h + 1])
                        m.then_inc(S["xc_ready"], 1)
                        after(act, "z_proj_ready", n)
                        m = nc.scalar.activation(silu_z[:, :, bass.ds(n, 1), :].rearrange("p h o t -> p h (o t)"),
                                                 ps[:, ZB:ZB + EH, :], ACT.Silu)
                        m.then_inc(S["z_ready"], 1)
                        after(act, "c_proj_ready", n)
                        nc.scalar.copy(c_feat[bb * N:(bb + 1) * N, bass.ds(q, 1), :].rearrange("p o t -> p (o t)"),
                                       ps[bb * N:(bb + 1) * N, CB, :]).then_inc(S["c_ready"], 1)
                        after(act, "v_ready", n)
                        after(act, "p_ready", n, back=1)
                        nc.scalar.activation(soft[:, 0], soft[:, 0], ACT.Exp).then_inc(S["exp_ready"], 1)
                        after(act, "p_ready", n)
                        nc.scalar.activation(soft[:, 0], soft[:, 1], ACT.Ln, bias=1.0).then_inc(S["ln_ready"], 1)
                        for kind, tok, rest, parts, ready in (("b", b_tok, b_rest, b_parts, "b_copied"),
                                                              ("dt", dt_tok, dt_rest, dt_parts, "dt_ready"),
                                                              ("u", u_tok, u_rest, u_parts, "u_ready")):
                            after(act, ready, n)
                            after(act, "parts_stored", n, per=16 * (2 * NP + NP * NP), back=1)
                            nc.scalar.copy(parts[:, 0], tok[:]).then_inc(S[kind + "_hi_ready"], 1)
                        for kind, rest, parts in (("b", b_rest, b_parts), ("dt", dt_rest, dt_parts),
                                                  ("u", u_rest, u_parts)):
                            after(act, kind + "_r1_ready", n)
                            nc.scalar.copy(parts[:, 1], rest[:]).then_inc(S[kind + "_mid_ready"], 1)

                    batches(act, body)

                @block.vector
                def _(dve):
                    dve.wait_ge(weights, NWEIGHTS)

                    def body(q, bb):
                        n = q * 2 + bb
                        dve.wait_ge(S[f"x_loaded{bb}"], (q + 1) * 16)
                        for j in range(NJ):
                            m = nc.vector.bn_stats(stats[:, bb, j], x_tok[:, bb, j])
                        m.then_inc(S["stats_ready"], 1)
                        after(dve, "stats_ready", n)
                        nc.vector.memset(wait_mark[:], 0.0)
                        for j in range(NJ):
                            m = nc.vector.bn_aggr(mean_var[:, bb, j], stats[:, bb, j])
                        m.then_inc(S["moments_ready"], 1)
                        after(dve, "rms_ready", n)
                        after(dve, "normed_t_ready", n, back=2)
                        for j in range(NJ):
                            m = nc.vector.tensor_scalar(normed[:, bb, j], x_tok[:, bb, j], mean_var[:, bb, j, 0:1],
                                                        nrm[:, 5, j:j + 1], ALU.subtract, ALU.mult)
                        m.then_inc(S["normed_ready"], 1)
                        after(dve, "tok_proj_ready", n)
                        after(dve, "ln_ready", n, back=1)
                        after(dve, "dt0_ready", n, back=1)
                        nc.vector.tensor_tensor(soft[:, 0], ps[:, TOK:TOK + NJ, 0:E],
                                                dtb_bc[:].unsqueeze(1).broadcast_to([P, NJ, E]), ALU.add
                                                ).then_inc(S["v_ready"], 1)
                        after(dve, "b_mid_ready", n, back=1)
                        nc.vector.tensor_copy(b_tok[:], ps[:, TOK:TOK + NJ, E:E + N]).then_inc(S["b_copied"], 1)
                        after(dve, "exp_ready", n)
                        nc.vector.tensor_scalar(soft[:, 1], soft[:, 0], 1.0, None, ALU.min).then_inc(S["w1_step"], 1)
                        dve.wait_ge(S["w1_step"], n + 1)
                        nc.vector.tensor_scalar(soft[:, 2], soft[:, 1], 1.0, -1.0, ALU.add, ALU.add
                                                ).then_inc(S["p_ready"], 1)
                        after(dve, "b_hi_ready", n)
                        nc.vector.tensor_tensor(b_rest[:], b_tok[:], b_parts[:, 0], ALU.subtract
                                                ).then_inc(S["b_r1_ready"], 1)
                        after(dve, "ln_ready", n)
                        after(dve, "log_err_ready", n)
                        after(dve, "dt_r1_ready", n, back=1)
                        nc.vector.tensor_tensor(soft[:, 0], soft[:, 0], soft[:, 3], ALU.subtract
                                                ).then_inc(S["dt0_ready"], 1)
                        after(dve, "dt0_ready", n)
                        nc.vector.tensor_scalar(dt_tok[:], soft[:, 0], DT_MIN, DT_MAX, ALU.max, ALU.min
                                                ).then_inc(S["dt_ready"], 1)
                        after(dve, "dt_ready", n)
                        after(dve, "xc_t_ready", n)
                        nc.vector.tensor_tensor(u_tok[:].rearrange("p j e -> p (j e)"),
                                                ps[:, XC:XC + 2, :].rearrange("p a c -> p (a c)"),
                                                dt_tok[:].rearrange("p j e -> p (j e)"), ALU.mult
                                                ).then_inc(S["u_ready"], 1)
                        after(dve, "b_mid_ready", n)
                        nc.vector.tensor_tensor(b_parts[:, 2], b_rest[:], b_parts[:, 1], ALU.subtract
                                                ).then_inc(S["b_split"], 1)
                        after(dve, "u_hi_ready", n)
                        nc.vector.tensor_tensor(u_rest[:], u_tok[:], u_parts[:, 0], ALU.subtract
                                                ).then_inc(S["u_r1_ready"], 1)
                        after(dve, "u_mid_ready", n)
                        nc.vector.tensor_tensor(u_parts[:, 2], u_rest[:], u_parts[:, 1], ALU.subtract
                                                ).then_inc(S["u_split"], 1)

                    batches(dve, body)

        with ExitStack() as c2:
            def pb(name, shape, dt=F32):
                return c2.enter_context(nc.sbuf_tensor(name, shape, dt))

            moving = pb("moving", [KROWS, 2, TC, E], BF16)
            b_rows = pb("b_rows", [KROWS, 2, TC, Q, P], BF16)
            dt_pick = pb("dt_pick", [KROWS, Q, P], BF16)
            c_cols = pb("c_cols", [P, 2, Q, TC * 2 * TC])
            decay = pb("decay", [P, RING, QE])
            state = pb("state", [P, RING, QE])
            decayed = pb("decayed", [P, SELF])

            chunk_loaded = [sem("chunk_loaded0"), sem("chunk_loaded1")]
            zeroed = sem("zeroed")
            start_zeroed = sem("start_zeroed")
            picks_ready = sem("picks_ready")
            dt_spread = sem("dt_spread")
            decay_ready = sem("decay_ready")
            self_decayed = sem("self_decayed")
            acc_decayed = sem("acc_decayed")
            self_input = sem("self_input")
            acc_state = sem("acc_state")
            self_state = sem("self_state")
            acc_copied = sem("acc_copied")
            contracted = sem("contracted")
            y_kept = sem("y_kept")
            c_placed = sem("c_placed")

            DTP, SELFP, ACCP, YP = 0, 2, 4, 6
            LOADS = 2 + Q * 2

            BODIES = T // STEPS

            def chunks(eng, body):
                for k in range(STEPS):
                    body(0, k)
                with eng.Fori(1, BODIES - 1) as i:
                    for k in range(STEPS):
                        body(i, k)
                for k in range(STEPS):
                    body(BODIES - 1, k)

            def known(t):
                return isinstance(t, int)

            def wait_step(eng, s, t):
                if known(t) and t < 0:
                    return
                eng.wait_ge(s, t + 1)

            with nc.Block() as block:
                @block.sync
                def _(sp):
                    def load(t, cb):
                        sp.dma_start(moving[0:UROWS, cb].rearrange("r t e -> r (t e)"),
                                     u_stage[:, :, bass.ds(t, TC), :].rearrange("i b t e -> (i b) (t e)")
                                     .unsqueeze(0).broadcast_to([NP, NP * B, TC * E])
                                     ).then_inc(chunk_loaded[cb], 16)
                        sp.dma_start(moving[UROWS:KROWS, cb].rearrange("r t e -> r (t e)"),
                                     dt_stage[:, :, bass.ds(t, TC), :].rearrange("i b t e -> (i b) (t e)")
                                     ).then_inc(chunk_loaded[cb], 16)
                        for b in range(B):
                            q, bb = b // 2, b % 2
                            sp.dma_start(b_rows[b:UROWS:B, cb, :, q, bb * N:(bb + 1) * N],
                                         b_stage[:, :, b, bass.ds(t, TC), :].rearrange("j i t n -> (j i) t n")
                                         ).then_inc(chunk_loaded[cb], 16)

                    sp.wait_ge(zeroed, 2)
                    load(0, 0)
                    load(TC, 1)
                    with sp.Fori(1, BODIES) as i:
                        for cb in range(2):
                            wait_all(sp, [(acc_state, i * STEPS + (cb + 1) * TC - STEPS + 1)])
                            load(i * STEPS + cb * TC, cb)

                @block.gpsimd
                def _(pool):
                    nc.gpsimd.memset(b_rows[:, 0], 0.0).then_inc(zeroed, 1)
                    nc.gpsimd.memset(b_rows[:, 1], 0.0).then_inc(zeroed, 1)
                    nc.gpsimd.memset(dt_pick[:], 0.0).then_inc(zeroed, 1)
                    nc.gpsimd.memset(c_cols[:], 0.0).then_inc(zeroed, 1)
                    pool.wait_ge(zeroed, 4)
                    for i in range(NP):
                        nc.gpsimd.affine_select(
                            out=dt_pick[:].rearrange("r q (b n) -> r q b n", b=2),
                            in_=dt_pick[:].rearrange("r q (b n) -> r q b n", b=2),
                            compare_op=ALU.not_equal, fill=1.0, base=-(UROWS + i * B),
                            pattern=[[-2, Q], [-1, 2], [0, N]], channel_multiplier=1).then_inc(picks_ready, 1)
                        pool.wait_ge(picks_ready, i + 1)

                    def place(i, cb):
                        t = i * STEPS + cb * TC
                        if not (known(i) and i == 0):
                            pool.wait_ge(contracted, t - TC)
                        for bb in range(2):
                            m = nc.gpsimd.tensor_copy(
                                c_cols[bb * N:(bb + 1) * N, cb, :, bb * TC:bb * TC + (TC - 1) * (2 * TC + 1) + 1:2 * TC + 1],
                                c_feat[bb * N:(bb + 1) * N, :, bass.ds(t, TC)])
                        m.then_inc(c_placed, 1)

                    place(0, 0)
                    place(0, 1)
                    with pool.Fori(1, BODIES) as i:
                        for cb in range(2):
                            place(i, cb)

                @block.tensor
                def _(pe):
                    for f in range(2):
                        for h in range(2):
                            m = nc.tensor.matmul(ps[:, ACCP + f, h * E:(h + 1) * E], zero_w[:, :], w_in[:, 0:E],
                                                 start=(h == 0), stop=(h == 1), skip_group_check=True)
                    m.then_inc(acc_state, 1)
                    pe.wait_ge(picks_ready, NP)

                    def spread_dt(i, k):
                        t = i * STEPS + k
                        if known(t) and t >= T:
                            return
                        cb, kk = (k // TC) % 2, k % TC
                        if kk == 0:
                            pe.wait_ge(chunk_loaded[cb], (i + k // STEPS + 1) * (16 * LOADS))
                        wait_step(pe, decay_ready, t - 1)
                        for q in range(Q):
                            m = nc.tensor.matmul(ps[:, DTP + q // 2, (q % 2) * E:(q % 2 + 1) * E], dt_pick[:, q, :],
                                                 moving[:, cb, kk, :], start=True, stop=True)
                        m.then_inc(dt_spread, 1)

                    def contract(i, k):
                        t = i * STEPS + k
                        if known(t) and t < 0:
                            return
                        cb, kk = (k // TC) % 2, k % TC
                        if kk == 0:
                            chunk = i * 2 + k // TC
                            pe.wait_ge(c_placed, chunk + 1)
                            if not (known(chunk) and chunk < 2):
                                pe.wait_ge(y_kept, chunk - 1)
                        wait_step(pe, self_state, t)
                        wait_step(pe, acc_copied, t)
                        for q in range(Q):
                            m = nc.tensor.matmul(ps[q * 32:(q + 1) * 32, YP + cb, 0:E],
                                                 c_cols[:, cb, q, kk * 2 * TC:(kk + 1) * 2 * TC],
                                                 state[:, k % RING, q * E:(q + 1) * E],
                                                 start=(kk == 0), stop=(kk == TC - 1))
                        m.then_inc(contracted, 1)

                    def step(i, k):
                        t = i * STEPS + k
                        cb, kk = (k // TC) % 2, k % TC
                        if known(t) and t == 0:
                            spread_dt(0, 0)
                            spread_dt(0, 1)
                        wait_step(pe, self_state, t - 2)
                        for q in range(Q // 2):
                            m = nc.tensor.matmul(ps[:, SELFP + k % 2, q * E:(q + 1) * E], b_rows[:, cb, kk, q, :],
                                                 moving[:, cb, kk, :], start=True, stop=True)
                        m.then_inc(self_input, 1)
                        spread_dt(i, k + 2)
                        wait_step(pe, acc_decayed, t)
                        for q in range(Q // 2, Q):
                            m = nc.tensor.matmul(ps[:, ACCP + k % 2, (q % 2) * E:(q % 2 + 1) * E],
                                                 b_rows[:, cb, kk, q, :], moving[:, cb, kk, :],
                                                 start=False, stop=False, skip_group_check=True)
                        m.then_inc(acc_state, 1)
                        contract(i, k - LAG)

                    chunks(pe, step)
                    for k in range(LAG):
                        contract(BODIES - 1, STEPS - LAG + k)

                @block.scalar
                def _(act):
                    act.wait_ge(a_ready, 1)

                    def exp_decay(i, k):
                        t = i * STEPS + k
                        if known(t) and t >= T:
                            return
                        wait_step(act, dt_spread, t)
                        wait_step(act, acc_decayed, t - RING)
                        wait_step(act, self_decayed, t - RING)
                        nc.scalar.activation(decay[:, k % RING, :], ps[:, DTP:DTP + 2, :].rearrange("p a c -> p (a c)"),
                                             ACT.Exp, scale=a_col[:, 2:3]).then_inc(decay_ready, 1)

                    def copy_state(i, k):
                        t = i * STEPS + k
                        if known(t) and t < 0:
                            return
                        act.wait_ge(acc_state, t + 2)
                        if not (known(t) and t == T - 1):
                            wait_step(act, acc_decayed, t + 1)
                        wait_step(act, contracted, t - RING)
                        nc.scalar.copy(state[:, k % RING, SELF:QE], ps[:, ACCP + k % 2, :]).then_inc(acc_copied, 1)

                    def step(i, k):
                        if known(i) and i == 0 and k == 0:
                            exp_decay(0, 0)
                            exp_decay(0, 1)
                        copy_state(i, k - 1)
                        exp_decay(i, k + 2)

                    chunks(act, step)
                    copy_state(BODIES - 1, STEPS - 1)

                @block.vector
                def _(dve):
                    nc.vector.memset(state[:, RING - 1, 0:SELF], 0.0).then_inc(start_zeroed, 1)

                    def step(i, k):
                        t = i * STEPS + k
                        wait_step(dve, decay_ready, t)
                        if known(t) and t == 0:
                            dve.wait_ge(start_zeroed, 1)
                        wait_step(dve, self_state, t - 1)
                        nc.vector.tensor_tensor(decayed[:], decay[:, k % RING, 0:SELF], state[:, (k - 1) % RING, 0:SELF],
                                                ALU.mult).then_inc(self_decayed, 1)
                        dve.wait_ge(acc_state, t + 1)
                        wait_step(dve, acc_copied, t - 2)
                        nc.vector.tensor_tensor(ps[:, ACCP + k % 2, :], decay[:, k % RING, SELF:QE],
                                                ps[:, ACCP + (k - 1) % 2, :], ALU.mult).then_inc(acc_decayed, 1)
                        wait_step(dve, self_decayed, t)
                        wait_step(dve, self_input, t)
                        wait_step(dve, contracted, t - RING)
                        nc.vector.tensor_tensor(state[:, k % RING, 0:SELF], decayed[:], ps[:, SELFP + k % 2, :],
                                                ALU.add).then_inc(self_state, 1)
                        if k % TC == LAG + 2 and not (known(t) and t < TC):
                            keep_y(i * 2 + k // TC - 1, (k // TC + 1) % 2)

                    def keep_y(chunk, cb):
                        dve.wait_ge(contracted, (chunk + 1) * TC)
                        nc.vector.tensor_copy(y_all[:, bass.ds(chunk, 1), :]
                                              .rearrange("p o e -> p (o e)"), ps[:, YP + cb, 0:E]).then_inc(y_kept, 1)

                    chunks(dve, step)
                    keep_y(NC - 1, 1)

        with ExitStack() as c3:
            def pb(name, shape, dt=F32):
                return c3.enter_context(nc.sbuf_tensor(name, shape, dt))

            x_in = pb("x_in", [P, 2, GT, D])
            y_in = pb("y_in", [P, 2, GT, E])
            f_stats = pb("f_stats", [P, GT, 6])
            f_mv = pb("f_mv", [P, GT, 2])
            f_nrm = pb("f_nrm", [P, 4, GT])
            square = pb("square", [P, GT, D])
            sumsq = pb("sumsq", [P, GT])
            xn = pb("xn", [P, GT, D])
            xn_feat = pb("xn_feat", [P, GTOK])
            gated = pb("gated", [P, EH, GTOK])
            x1 = pb("x1", [P, GT, D])
            base = pb("base", [P, GT, D])
            n2 = pb("n2", [P, GT, D])
            n2_feat = pb("n2_feat", [P, GTOK])
            gate_s = pb("gate_s", [P, IH, GTOK])
            hid = pb("hid", [P, IH, GTOK])
            h1 = pb("h1", [P, H1 // P, GTOK])
            h2 = pb("h2", [P, H2 // P, GTOK])
            result = pb("result", [P, 2, GT, D])

            names = ("f_x_loaded0 f_x_loaded1 f_y_loaded0 f_y_loaded1 f_stats_ready f_mv_ready f_rstd_ready f_xn_ready f_xn_t_ready "
                     "f_xn_feat_ready f_y_t_ready f_gated_ready f_proj_ready f_x1_ready f_sumsq_ready f_rrms_ready "
                     "f_n2_ready f_n2_t_ready f_n2_feat_ready f_gate_ready f_up_ready f_silu_ready f_hid_ready "
                     "f_h1_proj f_h1_ready f_h2_proj f_h2_ready f_base f_sum_ready f_result f_stored0 f_stored1 f_step")
            G = {n: sem(n) for n in names.split()}
            TR, TOKB, YT, UPB, HB = 0, 1, 2, 4, 4
            NHB = 4

            def after(eng, name, g, per=1, back=0):
                if isinstance(g, int) and g - back < 0:
                    return
                eng.wait_ge(G[name], (g - back + 1) * per)

            def groups(eng, body):
                for gb in range(2):
                    body(0, gb)
                with eng.Fori(1, NG // 2) as pair:
                    for gb in range(2):
                        body(pair, gb)

            with nc.Block() as block:
                @block.sync
                def _(sp):
                    def load(pair, gb):
                        g = pair * 2 + gb
                        wait_all(sp, [(G["f_base"], g - 1), (G["f_xn_ready"], g - 1)])
                        for j in range(GT):
                            sp.dma_start(x_in[:, gb, j, :], x[:, bass.ds(g * TG + j * TC, TC), :]
                                         ).then_inc(G[f"f_x_loaded{gb}"], 16)
                        wait_all(sp, [(G["f_y_t_ready"], g - 1)])
                        sp.dma_start(y_in[:, gb], y_all[:, bass.ds(g * GT, GT), :]).then_inc(G[f"f_y_loaded{gb}"], 16)

                    def store(pair, gb):
                        g = pair * 2 + gb
                        wait_all(sp, [(G["f_result"], g + 1)])
                        for j in range(GT):
                            sp.dma_start(out[:, bass.ds(g * TG + j * TC, TC), :], result[:, gb, j, :]
                                         ).then_inc(G[f"f_stored{gb}"], 16)

                    load(0, 0)
                    load(0, 1)
                    for gb in range(2):
                        store(0, gb)
                        load(1, gb)
                    with sp.Fori(1, NG // 2 - 1) as pair:
                        for gb in range(2):
                            store(pair, gb)
                            load(pair + 1, gb)
                    for gb in range(2):
                        store(NG // 2 - 1, gb)
                    for gb in range(2):
                        sp.wait_ge(G[f"f_stored{gb}"], 16 * GT * NG // 2)

                @block.gpsimd
                def _(pool):
                    def body(pair, gb):
                        g = pair * 2 + gb
                        after(pool, "f_mv_ready", g)
                        after(pool, "f_xn_ready", g, back=1)
                        nc.gpsimd.tensor_tensor(f_nrm[:, 0], f_mv[:, :, 1], eps_t[:], ALU.add).then_inc(G["f_step"], 1)
                        pool.wait_ge(G["f_step"], g * 3 + 1)
                        nc.gpsimd.tensor_tensor(f_nrm[:, 1], f_nrm[:, 0], mhalf[:], ALU.pow).then_inc(G["f_rstd_ready"], 1)
                        after(pool, "f_sumsq_ready", g)
                        after(pool, "f_n2_ready", g, back=1)
                        nc.gpsimd.tensor_tensor(f_nrm[:, 2], sumsq[:], inv_d[:], ALU.mult).then_inc(G["f_step"], 1)
                        pool.wait_ge(G["f_step"], g * 3 + 2)
                        nc.gpsimd.tensor_tensor(f_nrm[:, 2], f_nrm[:, 2], eps_t[:], ALU.add).then_inc(G["f_step"], 1)
                        pool.wait_ge(G["f_step"], g * 3 + 3)
                        nc.gpsimd.tensor_tensor(f_nrm[:, 3], f_nrm[:, 2], mhalf[:], ALU.pow).then_inc(G["f_rrms_ready"], 1)
                        after(pool, "f_x1_ready", g)
                        after(pool, "f_result", g, back=1)
                        nc.gpsimd.tensor_tensor(base[:], x_in[:, gb], x1[:], ALU.add).then_inc(G["f_base"], 1)

                    groups(pool, body)

                @block.tensor
                def _(pe):
                    def body(pair, gb):
                        g = pair * 2 + gb
                        after(pe, "f_xn_ready", g)
                        after(pe, "f_n2_feat_ready", g, back=1)
                        for j in range(GT):
                            m = nc.tensor.transpose(ps[:, TR, j * P:(j + 1) * P], xn[:, j], ident[:])
                        m.then_inc(G["f_xn_t_ready"], 1)
                        pe.wait_ge(G[f"f_y_loaded{gb}"], (pair + 1) * 16)
                        after(pe, "f_silu_ready", g, back=1)
                        for h in range(EH):
                            for j in range(GT):
                                m = nc.tensor.transpose(ps[:, YT + h, j * P:(j + 1) * P],
                                                        y_in[:, gb, j, h * P:(h + 1) * P], ident[:])
                        m.then_inc(G["f_y_t_ready"], 1)
                        after(pe, "f_xn_feat_ready", g)
                        after(pe, "f_hid_ready", g, back=1)
                        for m_ in range(H1 // P):
                            nc.tensor.matmul(ps[:, HB + m_, :], w0[:, m_ * P:(m_ + 1) * P], xn_feat[:],
                                             start=True, stop=True).then_inc(G["f_h1_proj"], 1)
                        after(pe, "f_gated_ready", g)
                        after(pe, "f_result", g, back=1)
                        for j in range(GT):
                            for h in range(EH):
                                m = nc.tensor.matmul(ps[:, TOKB, j * P:(j + 1) * P], gated[:, h, j * P:(j + 1) * P],
                                                     w_out[:, h, :], start=(h == 0), stop=(h == EH - 1))
                        m.then_inc(G["f_proj_ready"], 1)
                        after(pe, "f_h1_ready", g, per=H1 // P)
                        for m_ in range(H2 // P):
                            for c in range(H1 // P):
                                m = nc.tensor.matmul(ps[:, HB + m_, :], w1[:, c, m_ * P:(m_ + 1) * P], h1[:, c, :],
                                                     start=(c == 0), stop=(c == H1 // P - 1))
                            m.then_inc(G["f_h2_proj"], 1)
                        after(pe, "f_n2_ready", g)
                        after(pe, "f_xn_feat_ready", g)
                        for j in range(GT):
                            m = nc.tensor.transpose(ps[:, TR, j * P:(j + 1) * P], n2[:, j], ident[:])
                        m.then_inc(G["f_n2_t_ready"], 1)
                        after(pe, "f_n2_feat_ready", g)
                        after(pe, "f_gated_ready", g)
                        for h in range(IH):
                            m = nc.tensor.matmul(ps[:, YT + h, :], w_gate[:, h * P:(h + 1) * P], n2_feat[:],
                                                 start=True, stop=True)
                        m.then_inc(G["f_gate_ready"], 1)
                        after(pe, "f_h2_ready", g, per=H2 // P)
                        for h in range(IH):
                            m = nc.tensor.matmul(ps[:, UPB + h, :], w_up[:, h * P:(h + 1) * P], n2_feat[:],
                                                 start=True, stop=True)
                        m.then_inc(G["f_up_ready"], 1)
                        after(pe, "f_x1_ready", g)
                        after(pe, "f_hid_ready", g)
                        for j in range(GT):
                            js = slice(j * P, (j + 1) * P)
                            for c in range(H2 // P):
                                nc.tensor.matmul(ps[:, TOKB, js], h2[:, c, js], w2[:, c, :], start=(c == 0), stop=False)
                            for h in range(IH):
                                m = nc.tensor.matmul(ps[:, TOKB, js], hid[:, h, js], w_down[:, h, :],
                                                     start=False, stop=(h == IH - 1))
                        m.then_inc(G["f_sum_ready"], 1)

                    groups(pe, body)

                @block.scalar
                def _(act):
                    def body(pair, gb):
                        g = pair * 2 + gb
                        after(act, "f_xn_t_ready", g)
                        after(act, "f_h1_proj", g, per=H1 // P, back=1)
                        nc.scalar.copy(xn_feat[:], ps[:, TR, :]).then_inc(G["f_xn_feat_ready"], 1)
                        for m_ in range(H1 // P):
                            act.wait_ge(G["f_h1_proj"], g * (H1 // P) + m_ + 1)
                            after(act, "f_h2_proj", g, per=H2 // P, back=1)
                            nc.scalar.activation(h1[:, m_, :], ps[:, HB + m_, :], ACT.Relu, scale=s_col[:, 0:1]
                                                 ).then_inc(G["f_h1_ready"], 1)
                        after(act, "f_x1_ready", g)
                        after(act, "f_rrms_ready", g, back=1)
                        for j in range(GT):
                            m = nc.scalar.activation(square[:, j], x1[:, j], ACT.Square, accum_out=sumsq[:, j:j + 1])
                        m.then_inc(G["f_sumsq_ready"], 1)
                        after(act, "f_n2_t_ready", g)
                        after(act, "f_up_ready", g, back=1)
                        nc.scalar.activation(n2_feat[:], ps[:, TR, :], ACT.Copy, scale=fw_col[:, 0:1]
                                             ).then_inc(G["f_n2_feat_ready"], 1)
                        after(act, "f_gate_ready", g)
                        after(act, "f_hid_ready", g, back=1)
                        nc.scalar.activation(gate_s[:], ps[:, YT:YT + IH, :], ACT.Silu).then_inc(G["f_silu_ready"], 1)

                    groups(act, body)

                @block.vector
                def _(dve):
                    def body(pair, gb):
                        g = pair * 2 + gb
                        dve.wait_ge(G[f"f_x_loaded{gb}"], (pair + 1) * (16 * GT))
                        after(dve, "f_rstd_ready", g, back=1)
                        for j in range(GT):
                            m = nc.vector.bn_stats(f_stats[:, j], x_in[:, gb, j])
                        m.then_inc(G["f_stats_ready"], 1)
                        after(dve, "f_stats_ready", g)
                        nc.vector.memset(wait_mark[:], 0.0)
                        for j in range(GT):
                            m = nc.vector.bn_aggr(f_mv[:, j], f_stats[:, j])
                        m.then_inc(G["f_mv_ready"], 1)
                        after(dve, "f_rstd_ready", g)
                        after(dve, "f_xn_t_ready", g, back=1)
                        for j in range(GT):
                            m = nc.vector.tensor_scalar(xn[:, j], x_in[:, gb, j], f_mv[:, j, 0:1], f_nrm[:, 1, j:j + 1],
                                                        ALU.subtract, ALU.mult)
                        m.then_inc(G["f_xn_ready"], 1)
                        after(dve, "f_y_t_ready", g)
                        after(dve, "f_proj_ready", g, back=1)
                        for h in range(EH):
                            for j in range(GT):
                                m = nc.vector.tensor_tensor(
                                    gated[:, h, j * P:(j + 1) * P].rearrange("e (b t) -> e b t", b=B),
                                    ps[:, YT + h, j * P:(j + 1) * P].rearrange("e (b t) -> e b t", b=B),
                                    silu_z[:, h, :, bass.ds(g * TG + j * TC, TC)], ALU.mult)
                        m.then_inc(G["f_gated_ready"], 1)
                        after(dve, "f_proj_ready", g)
                        after(dve, "f_base", g, back=1)
                        after(dve, "f_n2_ready", g, back=1)
                        nc.vector.tensor_tensor(x1[:].rearrange("p j d -> p (j d)"), ps[:, TOKB, :],
                                                xn[:].rearrange("p j d -> p (j d)"), ALU.add).then_inc(G["f_x1_ready"], 1)
                        after(dve, "f_rrms_ready", g)
                        after(dve, "f_n2_t_ready", g, back=1)
                        for j in range(GT):
                            m = nc.vector.tensor_scalar(n2[:, j], x1[:, j], f_nrm[:, 3, j:j + 1], None, ALU.mult)
                        m.then_inc(G["f_n2_ready"], 1)
                        for m_ in range(H2 // P):
                            dve.wait_ge(G["f_h2_proj"], g * (H2 // P) + m_ + 1)
                            after(dve, "f_sum_ready", g, back=1)
                            nc.vector.tensor_scalar(h2[:, m_, :], ps[:, HB + m_, :], s_fold[:, 0:1], 0.0, ALU.mult, ALU.max
                                                    ).then_inc(G["f_h2_ready"], 1)
                        after(dve, "f_silu_ready", g)
                        after(dve, "f_up_ready", g)
                        nc.vector.tensor_tensor(hid[:], gate_s[:], ps[:, UPB:UPB + IH, :], ALU.mult
                                                ).then_inc(G["f_hid_ready"], 1)
                        after(dve, "f_sum_ready", g)
                        after(dve, "f_base", g)
                        if not (isinstance(pair, int) and pair == 0):
                            dve.wait_ge(G[f"f_stored{gb}"], pair * (16 * GT))
                        nc.vector.tensor_tensor(result[:, gb].rearrange("p j d -> p (j d)"), ps[:, TOKB, :],
                                                base[:].rearrange("p j d -> p (j d)"), ALU.add).then_inc(G["f_result"], 1)

                    groups(dve, body)


_INS = ["L0_attn_x", "L0_attn_input_norm_w", "L0_attn_ffn_norm_w", "L0_attn_in_proj_W", "L0_attn_conv_W",
        "L0_attn_conv_b", "L0_attn_dt_W", "L0_attn_dt_b", "L0_attn_B_W", "L0_attn_C_W", "L0_attn_A_log",
        "L0_attn_out_proj_W", "L0_attn_gate_W", "L0_attn_up_W", "L0_attn_down_W", "L0_ffn_k0", "L0_ffn_k1",
        "L0_ffn_k2", "L0_ffn_s0", "L0_ffn_s1", "L0_ffn_s2"]


def kernel(**inputs):
    import numpy as _np
    import concourse.bacc as _bacc
    from concourse import mybir as _mybir
    from concourse.bass_utils import run_bass_kernel_spmd as _run

    nc = _bacc.Bacc("TRN2", target_bir_lowering=False, num_devices=1)
    arrays, args = {}, []
    for name in _INS:
        a = _np.ascontiguousarray(inputs[name])
        if a.ndim == 0:
            a = a.reshape(1)
        arrays[f"in_{name}_dram"] = a
        args.append(nc.dram_tensor(f"in_{name}_dram", a.shape, _mybir.dt.from_np(a.dtype), kind="ExternalInput").ap())
    shape = tuple(inputs["L0_attn_x"].shape)
    args.append(nc.dram_tensor("out_0_dram", shape, _mybir.dt.from_np(_np.dtype("float32")), kind="ExternalOutput").ap())
    mamba_and_binary_mlp_block(nc, *args)
    r = _run(nc, [arrays], core_ids=[0])
    return r.results[0]["out_0_dram"]
```

```python
from contextlib import ExitStack

import concourse.bass as bass
from concourse import mybir

F32 = mybir.dt.float32
BF16 = mybir.dt.bfloat16
U8 = mybir.dt.uint8
ALU = mybir.AluOpType
ACT = mybir.ActivationFunctionType

P = 128
EPS = 1e-5
DT_MIN, DT_MAX = 0.001, 0.1


def mamba_and_binary_mlp_block(nc: bass.Bass, x, norm_w, ffn_w, in_w, conv_w, conv_b, dt_w, dt_b, b_w, c_w,
                               a_log, out_w, gate_w, up_w, down_w, k0, k1, k2, s0, s1, s2, out):
    B, T, D = x.shape
    E = in_w.shape[1] // 2
    N = a_log.shape[0]
    I = gate_w.shape[1]
    H1, H2 = k0.shape[1], k1.shape[1]
    EH = E // P
    IH = I // P
    NJ = T // P
    NP = 3
    Q = B // 2
    TAPS = conv_w.shape[0]
    PAD_L = (TAPS - 1) // 2
    TPAD = T + TAPS - 1
    assert D == P and 2 * N == P and T % P == 0

    TC = 16
    NC = T // TC
    UROWS = NP * NP * B
    KROWS = UROWS + NP * B
    QE = Q * E
    SELF = QE // 2
    RING = 4
    STEPS = 2 * TC
    LAG = 2

    TG = STEPS
    NG = T // TG
    BODIES = T // STEPS
    GT = TG // TC
    GTOK = GT * P

    u_stage = nc.dram_tensor("u_stage", (NP, B, T, E), BF16, kind="Internal").ap()
    dt_stage = nc.dram_tensor("dt_stage", (NP, B, T, E), BF16, kind="Internal").ap()
    b_stage = nc.dram_tensor("b_stage", (NP, NP, B, T, N), BF16, kind="Internal").ap()

    with ExitStack() as ctx:
        def sb(name, shape, dt=F32):
            return ctx.enter_context(nc.sbuf_tensor(name, shape, dt))

        def sem(name):
            return ctx.enter_context(nc.semaphore(name))

        ps = ctx.enter_context(nc.psum_tensor("ps", [P, 8, 512], F32))

        ident = sb("ident", [P, P])
        zero_w = sb("zero_w", [P, P])
        mhalf = sb("mhalf", [P, NJ])
        w_in = sb("w_in", [P, 2 * E])
        conv_bc = sb("conv_bc", [P, TAPS, E])
        w_tap = sb("w_tap", [P, TAPS, E])
        w_dtb = sb("w_dtb", [P, EH, E + N])
        w_c = sb("w_c", [P, EH, N])
        w_out = sb("w_out", [P, EH, D])
        w_gate = sb("w_gate", [P, I])
        w_up = sb("w_up", [P, I])
        w_down = sb("w_down", [P, IH, D])
        nw_col = sb("nw_col", [P, 1])
        fw_col = sb("fw_col", [P, 1])
        cb_col = sb("cb_col", [P, EH])
        dtb_bc = sb("dtb_bc", [P, E])
        a_col = sb("a_col", [P, 3])
        s_col = sb("s_col", [P, 3])
        s_fold = sb("s_fold", [P, 2])
        w0 = sb("w0", [P, H1])
        w1 = sb("w1", [P, H1 // P, H2])
        w2 = sb("w2", [P, H2 // P, D])

        silu_z = sb("silu_z", [P, EH, B, T])
        c_feat = sb("c_feat", [P, Q, T])
        b_rows = sb("b_rows", [KROWS, 2, TC, Q, P], BF16)
        dt_pick = sb("dt_pick", [KROWS, Q, P], BF16)
        c_cols = sb("c_cols", [P, 2, Q, TC * 2 * TC])

        wait_mark = sb("wait_mark", [P, 1])
        inv_d = sb("inv_d", [P, NJ])
        eps_t = sb("eps_t", [P, NJ])
        weights = sem("weights")
        const_zero = sem("const_zero")
        const_done = sem("const_done")
        taps_ready = sem("taps_ready")
        bin_raw = sem("bin_raw")
        bin_ready = sem("bin_ready")
        a_exp = sem("a_exp")
        a_ready = sem("a_ready")
        x_first_loaded = sem("x_first_loaded")
        x_rest_loaded = sem("x_rest_loaded")
        picks_zeroed = sem("picks_zeroed")
        picks_ready = sem("picks_ready")

        def settle(eng):
            eng.wait_ge(weights, NWEIGHTS)

        def wait_all(eng, waits):
            settle(eng)
            for s, v in waits:
                if not (isinstance(v, int) and v <= 0):
                    eng.wait_ge(s, v)

        c1 = ctx.enter_context(ExitStack())
        x_tok = c1.enter_context(nc.sbuf_tensor("x_tok", [P, B, NJ, D], F32))

        with ExitStack() as c0:
            k0_raw = c0.enter_context(nc.sbuf_tensor("k0_raw", [P, 2, H1], U8))
            k1_raw = c0.enter_context(nc.sbuf_tensor("k1_raw", [P, H1 // P, H2], U8))
            k2_raw = c0.enter_context(nc.sbuf_tensor("k2_raw", [P, H2 // P, D], U8))
            k0_f = c0.enter_context(nc.sbuf_tensor("k0_f", [P, H1], F32))
            with nc.Block() as block:
                loads = [
                    (w_in[:], in_w), (w_dtb[:, :, 0:E], dt_w.rearrange("(h p) e -> p h e", p=P)),
                    (w_dtb[:, :, E:E + N], b_w.rearrange("(h p) n -> p h n", p=P)),
                    (w_c[:], c_w.rearrange("(h p) n -> p h n", p=P)),
                    (w_out[:], out_w.rearrange("(h p) d -> p h d", p=P)),
                    (w_gate[:], gate_w), (w_up[:], up_w), (w_down[:], down_w.rearrange("(h p) d -> p h d", p=P)),
                    (k0_raw[:], k0.rearrange("(h p) f -> p h f", p=P)),
                    (k1_raw[:], k1.rearrange("(h p) f -> p h f", p=P)),
                    (k2_raw[:], k2.rearrange("(h p) f -> p h f", p=P)),
                    (conv_bc[:], conv_w.rearrange("k o e -> o k e").partition_broadcast(P).rearrange("p o k e -> p (o k) e")),
                    (dtb_bc[:], dt_b.partition_broadcast(P)),
                    (nw_col[:], norm_w.unsqueeze(1)), (fw_col[:], ffn_w.unsqueeze(1)),
                    (a_col[0:N, 0:1], a_log.unsqueeze(1)), (a_col[N:P, 0:1], a_log.unsqueeze(1)),
                    (s_col[:, 0:1], s0.partition_broadcast(P)), (s_col[:, 1:2], s1.partition_broadcast(P)),
                    (s_col[:, 2:3], s2.partition_broadcast(P)),
                ] + [(cb_col[:, h:h + 1], conv_b[h * P:(h + 1) * P].unsqueeze(1)) for h in range(EH)]
                NWEIGHTS = 16 * len(loads)

                @block.sync
                def _(sp):
                    for dst, src in loads:
                        sp.dma_start(dst, src, allow_slow_non_contiguous=True).then_inc(weights, 16)
                    tokens_in = x.rearrange("b (p j) d -> p b (j d)", j=NJ)
                    x_rows = x_tok[:].rearrange("p b j d -> p b (j d)")
                    sp.dma_start(x_rows[:, 0:2], tokens_in[:, 0:2]).then_inc(x_first_loaded, 16)
                    sp.dma_start(x_rows[:, 2:B], tokens_in[:, 2:B]).then_inc(x_rest_loaded, 16)
                    sp.wait_ge(weights, NWEIGHTS)

                @block.gpsimd
                def _(pool):
                    nc.gpsimd.memset(ident[:], 0.0).then_inc(const_zero, 1)
                    nc.gpsimd.memset(zero_w[:], 0.0)
                    nc.gpsimd.memset(mhalf[:], -0.5)
                    nc.gpsimd.memset(eps_t[:], EPS)
                    nc.gpsimd.memset(inv_d[:], 1.0 / D)
                    pool.wait_ge(const_zero, 1)
                    nc.gpsimd.affine_select(out=ident[:], in_=ident[:], compare_op=ALU.not_equal, fill=1.0, base=0,
                                            pattern=[[-1, P]], channel_multiplier=1).then_inc(const_done, 1)
                    nc.gpsimd.memset(dt_pick[:], 0.0).then_inc(picks_zeroed, 1)
                    pool.wait_ge(picks_zeroed, 1)
                    for i in range(NP):
                        nc.gpsimd.affine_select(
                            out=dt_pick[:].rearrange("r q (b n) -> r q b n", b=2),
                            in_=dt_pick[:].rearrange("r q (b n) -> r q b n", b=2),
                            compare_op=ALU.not_equal, fill=1.0, base=-(UROWS + i * B),
                            pattern=[[-2, Q], [-1, 2], [0, N]], channel_multiplier=1).then_inc(picks_ready, 1)
                        pool.wait_ge(picks_ready, i + 1)
                    nc.gpsimd.memset(b_rows[:, 0], 0.0)

                @block.scalar
                def _(act):
                    act.wait_ge(weights, NWEIGHTS)
                    nc.scalar.activation(a_col[:, 1:2], a_col[:, 0:1], ACT.Exp).then_inc(a_exp, 1)
                    act.wait_ge(a_exp, 1)
                    nc.scalar.mul(a_col[:, 2:3], a_col[:, 1:2], -1.0).then_inc(a_ready, 1)

                @block.vector
                def _(dve):
                    nc.vector.memset(c_cols[:], 0.0)
                    nc.vector.memset(b_rows[:, 1], 0.0)
                    dve.wait_ge(weights, NWEIGHTS)
                    for k in range(TAPS):
                        tap = nc.vector.tensor_tensor(w_tap[:, k, :], w_in[:, 0:E], conv_bc[:, k, :], ALU.mult)
                    tap.then_inc(taps_ready, 1)
                    nc.vector.tensor_copy(k0_f[:], k0_raw[:, 1, :]).then_inc(bin_raw, 1)
                    nc.vector.tensor_scalar(s_fold[:], s_col[:, 1:3], 2.0, None, ALU.mult).then_inc(bin_raw, 1)
                    nc.vector.tensor_scalar(w1[:], k1_raw[:], 2.0, -1.0, ALU.mult, ALU.add)
                    nc.vector.tensor_scalar(w2[:], k2_raw[:], 2.0, -1.0, ALU.mult, ALU.add).then_inc(bin_raw, 1)
                    dve.wait_ge(bin_raw, 3)
                    nc.vector.tensor_tensor(w0[:], k0_raw[:, 0, :], k0_f[:], ALU.subtract).then_inc(bin_raw, 1)
                    nc.vector.tensor_scalar(w2[:], w2[:], s_fold[:, 1:2], None, ALU.mult).then_inc(bin_ready, 1)
                    dve.wait_ge(bin_raw, 4)
                    nc.vector.tensor_scalar(w0[:], w0[:], 2.0, None, ALU.mult).then_inc(bin_ready, 1)

        with c1:
            def pb(name, shape, dt=F32):
                return c1.enter_context(nc.sbuf_tensor(name, shape, dt))

            stats = pb("stats", [P, 2, NJ, 6])
            mean_var = pb("mean_var", [P, 2, NJ, 2])
            nrm = pb("nrm", [P, 6, NJ])
            normed = pb("normed", [P, 2, NJ, D])
            n_feat = pb("n_feat", [P, 2, TPAD])
            xc_feat = pb("xc_feat", [P, 2, EH, T])
            soft = pb("soft", [P, 4, NJ, E])
            dt_tok = pb("dt_tok", [P, NJ, E])
            u_tok = pb("u_tok", [P, NJ, E])
            dt_rest = pb("dt_rest", [P, NJ, E])
            u_rest = pb("u_rest", [P, NJ, E])
            b_tok = pb("b_tok", [P, NJ, N])
            b_rest = pb("b_rest", [P, NJ, N])
            dt_parts = pb("dt_parts", [P, NP, NJ, E], BF16)
            u_parts = pb("u_parts", [P, NP, NJ, E], BF16)
            b_parts = pb("b_parts", [P, NP, NJ, N], BF16)

            names = ("stats_ready moments_ready rms_ready normed_ready normed_t_ready n_feat_ready "
                     "xc_proj_ready z_proj_ready xc_ready z_ready tok_proj_ready xc_t_ready b_proj_ready c_proj_ready c_ready "
                     "v_ready exp_ready p_ready ln_ready log_err_ready dt0_ready dt_ready u_ready "
                     "b_copied dt_split u_split b_split parts_stored pads_ready nrm_step split_step "
                     "dt_hi_ready u_hi_ready b_hi_ready dt_r1_ready u_r1_ready b_r1_ready dt_mid_ready u_mid_ready b_mid_ready w1_step")
            S = {n: sem(n) for n in names.split()}

            def batches(eng, slot):
                def run(q, bb):
                    def at(stage, d):
                        sq, sbb = q + (bb + d) // 2, (bb + d) % 2
                        if not isinstance(q, int) or 0 <= sq * 2 + sbb < B:
                            stage(sq, sbb)
                    slot(at)

                for s in range(-1, 4):
                    run(s // 2, s % 2)
                with eng.Fori(2, Q - 1) as q:
                    for bb in range(2):
                        run(q, bb)
                for s in range(B - 2, B + 2):
                    run(s // 2, s % 2)

            def after(eng, name, n, per=1, back=0):
                if isinstance(n, int) and n - back < 0:
                    return
                eng.wait_ge(S[name], (n - back + 1) * per)

            NRM, BT, XC, DTT, CB, XCT = 0, 1, 2, 4, 6, 6

            with nc.Block() as block:
                @block.sync
                def _(sp):
                    def store(q, bb):
                        n = q * 2 + bb
                        for parts, stage, split in ((dt_parts, dt_stage, "dt_split"), (u_parts, u_stage, "u_split")):
                            wait_all(sp, [(S[split], n + 1)])
                            for i in range(NP):
                                sp.dma_start(stage[i, bass.ds(n, 1)].rearrange("o (p j) e -> (o p) (j e)", j=NJ),
                                             parts[:, i].rearrange("p j e -> p (j e)")).then_inc(S["parts_stored"], 16)
                        wait_all(sp, [(S["b_split"], n + 1)])
                        for j in range(NP):
                            for i in range(NP):
                                sp.dma_start(b_stage[j, i, bass.ds(n, 1)].rearrange("o (p j) e -> (o p) (j e)", j=NJ),
                                             b_parts[:, j].rearrange("p j e -> p (j e)")).then_inc(S["parts_stored"], 16)

                    for bb in range(2):
                        store(0, bb)
                    with sp.Fori(1, Q) as q:
                        for bb in range(2):
                            store(q, bb)
                    sp.wait_ge(S["parts_stored"], 16 * B * (2 * NP + NP * NP))

                @block.gpsimd
                def _(pool):
                    nc.gpsimd.memset(n_feat[:, :, 0:PAD_L], 0.0)
                    nc.gpsimd.memset(n_feat[:, :, PAD_L + T:TPAD], 0.0).then_inc(S["pads_ready"], 1)

                    def norms(q, bb):
                        n = q * 2 + bb
                        after(pool, "moments_ready", n)
                        after(pool, "normed_ready", n, back=1)
                        var = mean_var[:, bb, :, 1]
                        steps = [
                            lambda: nc.gpsimd.tensor_tensor(nrm[:, 0], var, eps_t[:], ALU.add),
                            lambda: nc.gpsimd.tensor_tensor(nrm[:, 1], nrm[:, 0], mhalf[:], ALU.pow),
                            lambda: nc.gpsimd.tensor_tensor(nrm[:, 2], var, nrm[:, 1], ALU.mult),
                            lambda: nc.gpsimd.tensor_tensor(nrm[:, 3], nrm[:, 2], nrm[:, 1], ALU.mult),
                            lambda: nc.gpsimd.tensor_tensor(nrm[:, 3], nrm[:, 3], eps_t[:], ALU.add),
                            lambda: nc.gpsimd.tensor_tensor(nrm[:, 4], nrm[:, 3], mhalf[:], ALU.pow),
                        ]
                        for k, step in enumerate(steps):
                            step().then_inc(S["nrm_step"], 1)
                            pool.wait_ge(S["nrm_step"], n * len(steps) + k + 1)
                        nc.gpsimd.tensor_tensor(nrm[:, 5], nrm[:, 4], nrm[:, 1], ALU.mult).then_inc(S["rms_ready"], 1)

                    def log_err(q, bb):
                        n = q * 2 + bb
                        after(pool, "p_ready", n)
                        after(pool, "dt0_ready", n, back=1)
                        nc.gpsimd.tensor_tensor(soft[:, 3], soft[:, 2], soft[:, 1], ALU.subtract
                                                ).then_inc(S["log_err_ready"], 1)

                    def first_rest(q, bb):
                        n = q * 2 + bb
                        after(pool, "dt_hi_ready", n)
                        nc.gpsimd.tensor_tensor(dt_rest[:], dt_tok[:], dt_parts[:, 0], ALU.subtract
                                                ).then_inc(S["dt_r1_ready"], 1)

                    def second_rest(q, bb):
                        n = q * 2 + bb
                        after(pool, "dt_mid_ready", n)
                        nc.gpsimd.tensor_tensor(dt_parts[:, 2], dt_rest[:], dt_parts[:, 1], ALU.subtract
                                                ).then_inc(S["dt_split"], 1)

                    def slot(at):
                        at(norms, 1)
                        at(first_rest, -2)
                        at(log_err, -1)
                        at(second_rest, -2)

                    batches(pool, slot)

                @block.tensor
                def _(pe):
                    pe.wait_ge(const_done, 1)
                    pe.wait_ge(taps_ready, 1)

                    def transpose_normed(q, bb):
                        n = q * 2 + bb
                        after(pe, "normed_ready", n)
                        after(pe, "z_ready", n, back=1)
                        for j in range(NJ):
                            m = nc.tensor.transpose(ps[:, NRM, j * P:(j + 1) * P], normed[:, bb, j], ident[:])
                        m.then_inc(S["normed_t_ready"], 1)

                    def project(q, bb):
                        n = q * 2 + bb
                        after(pe, "n_feat_ready", n)
                        after(pe, "xc_ready", n, back=1)
                        for h in range(EH):
                            for k in range(TAPS):
                                m = nc.tensor.matmul(ps[:, XC + h, :], w_tap[:, k, h * P:(h + 1) * P],
                                                     n_feat[:, bb, k:k + T], start=(k == 0), stop=(k == TAPS - 1))
                            m.then_inc(S["xc_proj_ready"], 1)
                        after(pe, "b_copied", n, back=1)
                        for h in range(EH):
                            m = nc.tensor.matmul(ps[:, NRM + h, :], w_in[:, E + h * P:E + (h + 1) * P],
                                                 n_feat[:, bb, PAD_L:PAD_L + T], start=True, stop=True)
                        m.then_inc(S["z_proj_ready"], 1)

                    def dt_products(q, bb):
                        n = q * 2 + bb
                        after(pe, "xc_ready", n)
                        after(pe, "v_ready", n, back=1)
                        for j in range(NJ):
                            for h in range(EH):
                                m = nc.tensor.matmul(ps[:, DTT + j // 2, (j % 2) * E:(j % 2 + 1) * E],
                                                     xc_feat[:, bb, h, j:T:NJ], w_dtb[:, h, 0:E],
                                                     start=(h == 0), stop=(h == EH - 1))
                        m.then_inc(S["tok_proj_ready"], 1)

                    def bc_products(q, bb):
                        n = q * 2 + bb
                        after(pe, "u_ready", n, back=1)
                        for h in range(EH):
                            m = nc.tensor.matmul(ps[bb * N:(bb + 1) * N, CB, :], w_c[:, h, :], xc_feat[:, bb, h, :],
                                                 start=(h == 0), stop=(h == EH - 1))
                        m.then_inc(S["c_proj_ready"], 1)
                        after(pe, "z_ready", n)
                        for j in range(NJ):
                            for h in range(EH):
                                m = nc.tensor.matmul(ps[:, BT, j * N:(j + 1) * N],
                                                     xc_feat[:, bb, h, j:T:NJ], w_dtb[:, h, E:E + N],
                                                     start=(h == 0), stop=(h == EH - 1))
                        m.then_inc(S["b_proj_ready"], 1)
                        after(pe, "c_ready", n)
                        for j in range(NJ):
                            for h in range(EH):
                                m = nc.tensor.transpose(
                                    ps[:, XCT + j // 2, (j % 2) * E + h * P:(j % 2) * E + (h + 1) * P],
                                    xc_feat[:, bb, h, j:T:NJ], ident[:])
                        m.then_inc(S["xc_t_ready"], 1)

                    def slot(at):
                        at(dt_products, -1)
                        at(transpose_normed, 0)
                        at(bc_products, -1)
                        at(project, 0)

                    batches(pe, slot)

                @block.scalar
                def _(act):
                    act.wait_ge(weights, NWEIGHTS)
                    act.wait_ge(S["pads_ready"], 1)

                    def normed_to_sbuf(q, bb):
                        n = q * 2 + bb
                        after(act, "normed_t_ready", n)
                        after(act, "z_proj_ready", n, back=2)
                        nc.scalar.activation(
                            n_feat[:, bb, PAD_L:PAD_L + T].rearrange("d (p j) -> d p j", j=NJ),
                            ps[:, NRM, :].rearrange("d (j p) -> d p j", j=NJ), ACT.Copy, scale=nw_col[:, 0:1]
                        ).then_inc(S["n_feat_ready"], 1)

                    def silus(q, bb):
                        n = q * 2 + bb
                        after(act, "xc_t_ready", n, back=2)
                        for h in range(EH):
                            act.wait_ge(S["xc_proj_ready"], n * EH + h + 1)
                            m = nc.scalar.activation(xc_feat[:, bb, h, :], ps[:, XC + h, :], ACT.Silu,
                                                     bias=cb_col[:, h:h + 1])
                        m.then_inc(S["xc_ready"], 1)
                        after(act, "z_proj_ready", n)
                        m = nc.scalar.activation(silu_z[:, :, bass.ds(n, 1), :].rearrange("p h o t -> p h (o t)"),
                                                 ps[:, NRM:NRM + EH, :], ACT.Silu)
                        m.then_inc(S["z_ready"], 1)

                    def c_to_sbuf(q, bb):
                        n = q * 2 + bb
                        after(act, "c_proj_ready", n)
                        nc.scalar.copy(c_feat[bb * N:(bb + 1) * N, bass.ds(q, 1), :].rearrange("p o t -> p (o t)"),
                                       ps[bb * N:(bb + 1) * N, CB, :]).then_inc(S["c_ready"], 1)

                    def dt_exp(q, bb):
                        n = q * 2 + bb
                        after(act, "v_ready", n)
                        nc.scalar.activation(soft[:, 0], soft[:, 0], ACT.Exp).then_inc(S["exp_ready"], 1)

                    def dt_log(q, bb):
                        n = q * 2 + bb
                        after(act, "p_ready", n)
                        nc.scalar.activation(soft[:, 0], soft[:, 1], ACT.Ln, bias=1.0).then_inc(S["ln_ready"], 1)

                    def first_parts(q, bb):
                        n = q * 2 + bb
                        after(act, "parts_stored", n, per=16 * (2 * NP + NP * NP), back=1)
                        for kind, tok, parts, ready in (("dt", dt_tok, dt_parts, "dt_ready"),
                                                        ("u", u_tok, u_parts, "u_ready"),
                                                        ("b", b_tok, b_parts, "b_copied")):
                            after(act, ready, n)
                            nc.scalar.copy(parts[:, 0], tok[:]).then_inc(S[kind + "_hi_ready"], 1)

                    def second_parts(q, bb):
                        n = q * 2 + bb
                        for kind, rest, parts in (("u", u_rest, u_parts), ("b", b_rest, b_parts),
                                                  ("dt", dt_rest, dt_parts)):
                            after(act, kind + "_r1_ready", n)
                            nc.scalar.copy(parts[:, 1], rest[:]).then_inc(S[kind + "_mid_ready"], 1)

                    def slot(at):
                        at(first_parts, -2)
                        at(normed_to_sbuf, 0)
                        at(c_to_sbuf, -1)
                        at(dt_exp, -1)
                        at(second_parts, -2)
                        at(dt_log, -1)
                        at(silus, 0)

                    batches(act, slot)

                @block.vector
                def _(dve):
                    dve.wait_ge(weights, NWEIGHTS)

                    def moments(q, bb):
                        n = q * 2 + bb
                        if not isinstance(n, int) or n < 2:
                            dve.wait_ge(x_first_loaded, 16)
                        if not isinstance(n, int) or n >= 2:
                            dve.wait_ge(x_rest_loaded, 16)
                        for j in range(NJ):
                            m = nc.vector.bn_stats(stats[:, bb, j], token_tile(n, j))
                        m.then_inc(S["stats_ready"], 1)
                        after(dve, "stats_ready", n)
                        nc.vector.memset(wait_mark[:], 0.0)
                        for j in range(NJ):
                            m = nc.vector.bn_aggr(mean_var[:, bb, j], stats[:, bb, j])
                        m.then_inc(S["moments_ready"], 1)

                    def token_tile(n, j):
                        return x_tok[:, bass.ds(n, 1), j].rearrange("p o d -> p (o d)")

                    def normalize(q, bb):
                        n = q * 2 + bb
                        after(dve, "rms_ready", n)
                        after(dve, "normed_t_ready", n, back=2)
                        for j in range(NJ):
                            m = nc.vector.tensor_scalar(normed[:, bb, j], token_tile(n, j), mean_var[:, bb, j, 0:1],
                                                        nrm[:, 5, j:j + 1], ALU.subtract, ALU.mult)
                        m.then_inc(S["normed_ready"], 1)

                    def dt_bias(q, bb):
                        n = q * 2 + bb
                        after(dve, "tok_proj_ready", n)
                        after(dve, "dt0_ready", n, back=1)
                        nc.vector.tensor_tensor(soft[:, 0],
                                                ps[:, DTT:DTT + 2, :].rearrange("p a (c e) -> p (a c) e", c=2),
                                                dtb_bc[:].unsqueeze(1).broadcast_to([P, NJ, E]), ALU.add
                                                ).then_inc(S["v_ready"], 1)

                    def b_to_sbuf(q, bb):
                        n = q * 2 + bb
                        after(dve, "b_proj_ready", n)
                        after(dve, "b_r1_ready", n, back=1)
                        nc.vector.tensor_copy(b_tok[:].rearrange("p j n -> p (j n)"), ps[:, BT, 0:NJ * N]
                                              ).then_inc(S["b_copied"], 1)

                    def exp_to_p(q, bb):
                        n = q * 2 + bb
                        after(dve, "exp_ready", n)
                        after(dve, "log_err_ready", n, back=1)
                        nc.vector.tensor_scalar(soft[:, 1], soft[:, 0], 1.0, None, ALU.min).then_inc(S["w1_step"], 1)
                        dve.wait_ge(S["w1_step"], n + 1)
                        nc.vector.tensor_scalar(soft[:, 2], soft[:, 1], 1.0, -1.0, ALU.add, ALU.add
                                                ).then_inc(S["p_ready"], 1)

                    def dt_and_u(q, bb):
                        n = q * 2 + bb
                        after(dve, "ln_ready", n)
                        after(dve, "log_err_ready", n)
                        nc.vector.tensor_tensor(soft[:, 0], soft[:, 0], soft[:, 3], ALU.subtract
                                                ).then_inc(S["dt0_ready"], 1)
                        after(dve, "dt0_ready", n)
                        after(dve, "dt_r1_ready", n, back=1)
                        nc.vector.tensor_scalar(dt_tok[:], soft[:, 0], DT_MIN, DT_MAX, ALU.max, ALU.min
                                                ).then_inc(S["dt_ready"], 1)
                        after(dve, "dt_ready", n)
                        after(dve, "xc_t_ready", n)
                        after(dve, "u_r1_ready", n, back=1)
                        nc.vector.tensor_tensor(u_tok[:].rearrange("p j e -> p (j e)"),
                                                ps[:, XCT:XCT + 2, :].rearrange("p a c -> p (a c)"),
                                                dt_tok[:].rearrange("p j e -> p (j e)"), ALU.mult
                                                ).then_inc(S["u_ready"], 1)

                    def first_rests(q, bb):
                        n = q * 2 + bb
                        after(dve, "u_hi_ready", n)
                        nc.vector.tensor_tensor(u_rest[:], u_tok[:], u_parts[:, 0], ALU.subtract
                                                ).then_inc(S["u_r1_ready"], 1)
                        after(dve, "b_hi_ready", n)
                        nc.vector.tensor_tensor(b_rest[:], b_tok[:], b_parts[:, 0], ALU.subtract
                                                ).then_inc(S["b_r1_ready"], 1)

                    def second_rests(q, bb):
                        n = q * 2 + bb
                        after(dve, "u_mid_ready", n)
                        nc.vector.tensor_tensor(u_parts[:, 2], u_rest[:], u_parts[:, 1], ALU.subtract
                                                ).then_inc(S["u_split"], 1)
                        after(dve, "b_mid_ready", n)
                        nc.vector.tensor_tensor(b_parts[:, 2], b_rest[:], b_parts[:, 1], ALU.subtract
                                                ).then_inc(S["b_split"], 1)

                    def slot(at):
                        at(moments, 1)
                        at(first_rests, -2)
                        at(dt_bias, -1)
                        at(normalize, 1)
                        at(b_to_sbuf, -1)
                        at(exp_to_p, -1)
                        at(second_rests, -2)
                        at(dt_and_u, -1)

                    batches(dve, slot)

        with ExitStack() as c2:
            def pb(name, shape, dt=F32):
                return c2.enter_context(nc.sbuf_tensor(name, shape, dt))

            moving = pb("moving", [KROWS, 2, TC, E], BF16)
            decay = pb("decay", [P, RING, QE])
            state = pb("state", [P, RING, QE])
            decayed = pb("decayed", [P, Q // 2, E])

            x_in = pb("x_in", [P, GT, D])
            y_tok = pb("y_tok", [P, GT, E])
            f_stats = pb("f_stats", [P, GT, 6])
            f_mv = pb("f_mv", [P, GT, 2])
            f_nrm = pb("f_nrm", [P, 4, GT])
            square = pb("square", [P, GT, D])
            sumsq = pb("sumsq", [P, GT])
            xn = pb("xn", [P, GT, D])
            xn_feat = pb("xn_feat", [P, GTOK])
            gated = pb("gated", [P, EH, GTOK])
            x1 = pb("x1", [P, GT, D])
            base = pb("base", [P, GT, D])
            n2 = pb("n2", [P, GT, D])
            n2_feat = pb("n2_feat", [P, GTOK])
            h1 = pb("h1", [P, H1 // P, GTOK])
            h2 = pb("h2", [P, H2 // P, GTOK])
            gate_tanh = pb("gate_tanh", [P, IH, GTOK])
            gate_s = pb("gate_s", [P, IH, GTOK])
            hid = pb("hid", [P, IH, GTOK])
            result = pb("result", [P, GT, D])
            names = ("f_x_loaded f_stats_ready f_mv_ready f_rstd_ready f_xn_ready f_xn_t_ready f_xn_feat_ready "
                     "f_y_t_ready f_gated_ready f_proj_ready f_x1_ready f_sumsq_ready f_rrms_ready f_n2_ready "
                     "f_n2_t_ready f_n2_feat_ready f_h1_proj f_h1_ready f_h2_proj f_h2_ready f_gate_ready "
                     "f_gate_tanh_ready f_silu_ready f_up_ready f_hid_ready f_sum_ready f_base "
                     "f_result f_stored f_step")
            G = {n: sem(n) for n in names.split()}

            K_STATS, K_RSTD, K_XN, K_XN_T, K_XN_FEAT = 0, 1, 3, 4, 5
            K_Y_T, K_GATED, K_OUT, K_X1, K_SQUARE, K_RRMS, K_BASE, K_N2 = 6, 7, 9, 11, 12, 13, 14, 15
            K_N2_T, K_N2_FEAT = 17, 18
            K_GATE, K_GATE_TANH, K_SILU, K_UP, K_HID = 22, 24, 25, (30, 32), 33
            K_H1, K_H1_RELU = (7, 11), (9, 13)
            K_H2, K_H2_RELU = (14, 24), (22, 32)
            K_LAST, K_RESULT = 33, 37
            H2_STEPS, LAST_STEPS = 8, 4

            def finish_groups(finish, i, k):
                if not (isinstance(i, int) and i < 2):
                    finish(i - 2, STEPS + k)
                if not (isinstance(i, int) and i < 1):
                    finish(i - 1, k)

            def finish_last(finish):
                for k in range(STEPS):
                    finish_groups(finish, BODIES, k)
                for k in range(STEPS, K_RESULT + 1):
                    finish(NG - 1, k)

            def after(eng, name, g, per=1, back=0):
                if isinstance(g, int) and g - back < 0:
                    return
                eng.wait_ge(G[name], (g - back + 1) * per)

            def share(items, part, parts):
                n = -(-len(items) // parts)
                return items[part * n:(part + 1) * n]

            chunk_loaded = [sem("chunk_loaded0"), sem("chunk_loaded1")]
            start_zeroed = sem("start_zeroed")
            self_dt_spread = sem("self_dt_spread")
            acc_dt_spread = sem("acc_dt_spread")
            self_decay_ready = sem("self_decay_ready")
            acc_decay_ready = sem("acc_decay_ready")
            self_decayed = [sem(f"self_decayed{p}") for p in range(Q // 2)]
            acc_decayed = sem("acc_decayed")
            self_input = sem("self_input")
            acc_state = sem("acc_state")
            self_state = [sem(f"self_state{p}") for p in range(Q // 2)]
            acc_copied = sem("acc_copied")
            contracted = sem("contracted")
            y_kept = sem("y_kept")
            c_placed = sem("c_placed")

            DTP, SELFP, FA, ACCP, YP, FB = 0, 2, 3, 4, 6, 7
            LOADS = 2 + Q * 2

            def chunks(eng, body):
                for i in range(3):
                    for k in range(STEPS):
                        body(i, k)
                with eng.Fori(3, BODIES - 1) as i:
                    for k in range(STEPS):
                        body(i, k)
                for k in range(STEPS):
                    body(BODIES - 1, k)

            def known(t):
                return isinstance(t, int)

            def wait_step(eng, s, t):
                if known(t) and t < 0:
                    return
                eng.wait_ge(s, t + 1)

            with nc.Block() as block:
                @block.sync
                def _(sp):
                    def load(t, cb):
                        sp.dma_start(moving[0:UROWS, cb].rearrange("r t e -> r (t e)"),
                                     u_stage[:, :, bass.ds(t, TC), :].rearrange("i b t e -> (i b) (t e)")
                                     .unsqueeze(0).broadcast_to([NP, NP * B, TC * E])
                                     ).then_inc(chunk_loaded[cb], 16)
                        sp.dma_start(moving[UROWS:KROWS, cb].rearrange("r t e -> r (t e)"),
                                     dt_stage[:, :, bass.ds(t, TC), :].rearrange("i b t e -> (i b) (t e)")
                                     ).then_inc(chunk_loaded[cb], 16)
                        for b in range(B):
                            q, bb = b // 2, b % 2
                            sp.dma_start(b_rows[b:UROWS:B, cb, :, q, bb * N:(bb + 1) * N],
                                         b_stage[:, :, b, bass.ds(t, TC), :].rearrange("j i t n -> (j i) t n")
                                         ).then_inc(chunk_loaded[cb], 16)

                    load(0, 0)
                    load(TC, 1)
                    def load_tokens(g):
                        if not (known(g) and g == 0):
                            wait_all(sp, [(G["f_base"], g)])
                        for j in range(GT):
                            sp.dma_start(x_in[:, j, :], x[:, bass.ds(g * TG + j * TC, TC), :]
                                         ).then_inc(G["f_x_loaded"], 16)

                    def store(g):
                        wait_all(sp, [(G["f_result"], g + 1)])
                        for j in range(GT):
                            sp.dma_start(out[:, bass.ds(g * TG + j * TC, TC), :], result[:, j, :]
                                         ).then_inc(G["f_stored"], 16)

                    def body(i):
                        if not (known(i) and i < 3):
                            store(i - 3)
                        for cb in range(2):
                            wait_all(sp, [(acc_state, i * STEPS + (cb + 1) * TC - STEPS + 1)])
                            load(i * STEPS + cb * TC, cb)
                            if cb == 0:
                                load_tokens(i - 1)

                    body(1)
                    body(2)
                    with sp.Fori(3, BODIES) as i:
                        body(i)
                    store(NG - 3)
                    load_tokens(NG - 1)
                    store(NG - 2)
                    store(NG - 1)
                    sp.wait_ge(G["f_stored"], 16 * GT * NG)

                @block.gpsimd
                def _(pool):
                    def decay_self(i, k):
                        t = i * STEPS + k
                        wait_step(pool, self_decay_ready, t)
                        if known(t) and t == 0:
                            pool.wait_ge(start_zeroed, 1)
                        for p in range(Q // 2):
                            wait_step(pool, self_state[p], t - 1)
                            nc.gpsimd.tensor_tensor(decayed[:, p], decay[:, k % RING, p * E:(p + 1) * E],
                                                    state[:, (k - 1) % RING, p * E:(p + 1) * E], ALU.mult
                                                    ).then_inc(self_decayed[p], 1)

                    def finish(g, k):
                        if k == K_RSTD:
                            after(pool, "f_mv_ready", g)
                            after(pool, "f_xn_ready", g, back=1)
                            nc.gpsimd.tensor_tensor(f_nrm[:, 0], f_mv[:, :, 1], eps_t[:, 0:GT], ALU.add
                                                    ).then_inc(G["f_step"], 1)
                            pool.wait_ge(G["f_step"], g * 3 + 1)
                            nc.gpsimd.tensor_tensor(f_nrm[:, 1], f_nrm[:, 0], mhalf[:, 0:GT], ALU.pow
                                                    ).then_inc(G["f_rstd_ready"], 1)
                        if k == K_RRMS:
                            after(pool, "f_sumsq_ready", g)
                            after(pool, "f_n2_ready", g, back=1)
                            nc.gpsimd.tensor_tensor(f_nrm[:, 2], sumsq[:], inv_d[:, 0:GT], ALU.mult
                                                    ).then_inc(G["f_step"], 1)
                            pool.wait_ge(G["f_step"], g * 3 + 2)
                            nc.gpsimd.tensor_tensor(f_nrm[:, 2], f_nrm[:, 2], eps_t[:, 0:GT], ALU.add
                                                    ).then_inc(G["f_step"], 1)
                            pool.wait_ge(G["f_step"], g * 3 + 3)
                            nc.gpsimd.tensor_tensor(f_nrm[:, 3], f_nrm[:, 2], mhalf[:, 0:GT], ALU.pow
                                                    ).then_inc(G["f_rrms_ready"], 1)
                        if k == K_BASE:
                            after(pool, "f_x1_ready", g)
                            after(pool, "f_result", g, back=1)
                            nc.gpsimd.tensor_tensor(base[:], x_in[:], x1[:], ALU.add).then_inc(G["f_base"], 1)

                    def step(i, k):
                        decay_self(i, k)
                        finish_groups(finish, i, k)

                    chunks(pool, step)
                    finish_last(finish)

                @block.tensor
                def _(pe):
                    for f in range(2):
                        for h in range(2):
                            m = nc.tensor.matmul(ps[:, ACCP + f, h * E:(h + 1) * E], zero_w[:, :], w_in[:, 0:E],
                                                 start=(h == 0), stop=(h == 1), skip_group_check=True)
                    m.then_inc(acc_state, 1)
                    pe.wait_ge(picks_ready, NP)

                    def spread_dt(i, k, pairs, ready, spread):
                        t = i * STEPS + k
                        if known(t) and t >= T:
                            return
                        cb, kk = (k // TC) % 2, k % TC
                        if kk == 0 and spread is self_dt_spread:
                            pe.wait_ge(chunk_loaded[cb], (i + k // STEPS + 1) * (16 * LOADS))
                        wait_step(pe, ready, t - 1)
                        for q in pairs:
                            m = nc.tensor.matmul(ps[:, DTP + q // 2, (q % 2) * E:(q % 2 + 1) * E], dt_pick[:, q, :],
                                                 moving[:, cb, kk, :], start=True, stop=True)
                        m.then_inc(spread, 1)

                    def spread_self(i, k):
                        spread_dt(i, k, range(Q // 2), self_decay_ready, self_dt_spread)

                    def spread_acc(i, k):
                        spread_dt(i, k, range(Q // 2, Q), acc_decay_ready, acc_dt_spread)

                    def contract(i, k):
                        t = i * STEPS + k
                        if known(t) and t < 0:
                            return
                        cb, kk = (k // TC) % 2, k % TC
                        if kk == 0:
                            chunk = i * 2 + k // TC
                            pe.wait_ge(c_placed, chunk + 1)
                            if not (known(chunk) and chunk < 1):
                                pe.wait_ge(y_kept, chunk)
                        wait_step(pe, self_state[1], t)
                        wait_step(pe, acc_copied, t)
                        for q in range(Q):
                            m = nc.tensor.matmul(ps[q * 32:(q + 1) * 32, YP, 0:E],
                                                 c_cols[:, cb, q, kk * 2 * TC:(kk + 1) * 2 * TC],
                                                 state[:, k % RING, q * E:(q + 1) * E],
                                                 start=(kk == 0), stop=(kk == TC - 1))
                        m.then_inc(contracted, 1)

                    def step(i, k):
                        t = i * STEPS + k
                        cb, kk = (k // TC) % 2, k % TC
                        if known(t) and t == 0:
                            for first in range(2):
                                spread_self(0, first)
                                spread_acc(0, first)
                            self_product(0, 0)
                        spread_self(i, k + 2)
                        wait_step(pe, acc_decayed, t)
                        for q in range(Q // 2, Q):
                            m = nc.tensor.matmul(ps[:, ACCP + k % 2, (q % 2) * E:(q % 2 + 1) * E],
                                                 b_rows[:, cb, kk, q, :], moving[:, cb, kk, :],
                                                 start=False, stop=False, skip_group_check=True)
                        m.then_inc(acc_state, 1)
                        spread_acc(i, k + 2)
                        contract(i, k - LAG)
                        self_product(i, k + 1)
                        finish_groups(finish, i, k)

                    def self_product(i, k):
                        t = i * STEPS + k
                        if known(t) and t >= T:
                            return
                        cb, kk = (k // TC) % 2, k % TC
                        wait_step(pe, self_state[1], t - 1)
                        for q in range(Q // 2):
                            m = nc.tensor.matmul(ps[:, SELFP, q * E:(q + 1) * E], b_rows[:, cb, kk, q, :],
                                                 moving[:, cb, kk, :], start=True, stop=True)
                        m.then_inc(self_input, 1)

                    def finish(g, k):
                        if k == K_XN_T:
                            after(pe, "f_xn_ready", g)
                            after(pe, "f_hid_ready", g, back=1)
                            for j in range(GT):
                                m = nc.tensor.transpose(ps[:, FA, j * P:(j + 1) * P], xn[:, j], ident[:])
                            m.then_inc(G["f_xn_t_ready"], 1)
                        if k == K_Y_T:
                            pe.wait_ge(y_kept, (g + 1) * GT)
                            after(pe, "f_xn_feat_ready", g)
                            for h in range(EH):
                                for j in range(GT):
                                    m = nc.tensor.transpose(ps[:, FA, (h * GT + j) * P:(h * GT + j + 1) * P],
                                                            y_tok[:, j, h * P:(h + 1) * P], ident[:])
                            m.then_inc(G["f_y_t_ready"], 1)
                        j = k - K_OUT
                        if 0 <= j < GT:
                            if j == 0:
                                after(pe, "f_gated_ready", g)
                            for h in range(EH):
                                m = nc.tensor.matmul(ps[:, FA, j * P:(j + 1) * P], gated[:, h, j * P:(j + 1) * P],
                                                     w_out[:, h, :], start=(h == 0), stop=(h == EH - 1))
                            if j == GT - 1:
                                m.then_inc(G["f_proj_ready"], 1)
                        for r in range(2):
                            c = k - K_H1[r]
                            if 0 <= c < 2:
                                if c == 0 and r == 0:
                                    after(pe, "f_xn_feat_ready", g)
                                    after(pe, "f_result", g, back=1)
                                elif c == 0:
                                    pe.wait_ge(G["f_h1_ready"], g * 2 + r)
                                f = (2 * r + c) * P
                                m = nc.tensor.matmul(ps[:, FB, c * GTOK:(c + 1) * GTOK], w0[:, f:f + P], xn_feat[:],
                                                     start=True, stop=True)
                                if c == 1:
                                    m.then_inc(G["f_h1_proj"], 1)
                        if k == K_N2_T:
                            after(pe, "f_n2_ready", g)
                            for j in range(GT):
                                m = nc.tensor.transpose(ps[:, FA, j * P:(j + 1) * P], n2[:, j], ident[:])
                            m.then_inc(G["f_n2_t_ready"], 1)
                        h = k - K_GATE
                        if 0 <= h < IH:
                            if h == 0:
                                after(pe, "f_n2_feat_ready", g)
                            m = nc.tensor.matmul(ps[:, FA, h * GTOK:(h + 1) * GTOK], w_gate[:, h * P:(h + 1) * P],
                                                 n2_feat[:], start=True, stop=True)
                            if h == IH - 1:
                                m.then_inc(G["f_gate_ready"], 1)
                        if k in K_UP:
                            h = K_UP.index(k)
                            if h == 0:
                                after(pe, "f_silu_ready", g)
                            m = nc.tensor.matmul(ps[:, FA, h * GTOK:(h + 1) * GTOK], w_up[:, h * P:(h + 1) * P],
                                                 n2_feat[:], start=True, stop=True)
                            if h == IH - 1:
                                m.then_inc(G["f_up_ready"], 1)
                        for r in range(2):
                            part = k - K_H2[r]
                            if 0 <= part < H2_STEPS:
                                if part == 0 and r == 0:
                                    after(pe, "f_h1_ready", g, per=2)
                                elif part == 0:
                                    pe.wait_ge(G["f_h2_ready"], g * 2 + r)
                                for c, n in share([(c, n) for c in range(2) for n in range(H1 // P)], part, H2_STEPS):
                                    f = (2 * r + c) * P
                                    m = nc.tensor.matmul(ps[:, FB, c * GTOK:(c + 1) * GTOK], w1[:, n, f:f + P],
                                                         h1[:, n, :], start=(n == 0), stop=(n == H1 // P - 1))
                                if part == H2_STEPS - 1:
                                    m.then_inc(G["f_h2_proj"], 1)
                        part = k - K_LAST
                        if 0 <= part < LAST_STEPS:
                            if part == 0:
                                after(pe, "f_h2_ready", g, per=2)
                            if part == 1:
                                after(pe, "f_hid_ready", g)
                            terms = ([(h2[:, c], w2[:, c, :]) for c in range(H2 // P)]
                                     + [(hid[:, h], w_down[:, h, :]) for h in range(IH)])
                            for j, c in share([(j, c) for j in range(GT) for c in range(len(terms))], part, LAST_STEPS):
                                m = nc.tensor.matmul(ps[:, FB, j * P:(j + 1) * P], terms[c][0][:, j * P:(j + 1) * P],
                                                     terms[c][1], start=(c == 0), stop=(c == len(terms) - 1))
                            if part == LAST_STEPS - 1:
                                m.then_inc(G["f_sum_ready"], 1)

                    chunks(pe, step)
                    for k in range(LAG):
                        contract(BODIES - 1, STEPS - LAG + k)
                    finish_last(finish)

                @block.scalar
                def _(act):
                    act.wait_ge(a_ready, 1)

                    def exp_decay(i, k):
                        t = i * STEPS + k
                        if known(t) and t >= T:
                            return
                        for f, spread, ready, used in ((0, self_dt_spread, self_decay_ready, self_decayed[1]),
                                                       (1, acc_dt_spread, acc_decay_ready, acc_decayed)):
                            wait_step(act, spread, t)
                            wait_step(act, used, t - RING)
                            nc.scalar.activation(decay[:, k % RING, f * SELF:(f + 1) * SELF], ps[:, DTP + f, :],
                                                 ACT.Exp, scale=a_col[:, 2:3]).then_inc(ready, 1)

                    def copy_state(i, k):
                        t = i * STEPS + k
                        if known(t) and t < 0:
                            return
                        act.wait_ge(acc_state, t + 2)
                        if not (known(t) and t == T - 1):
                            wait_step(act, acc_decayed, t + 1)
                        wait_step(act, contracted, t - RING)
                        nc.scalar.copy(state[:, k % RING, SELF:QE], ps[:, ACCP + k % 2, :]).then_inc(acc_copied, 1)

                    def step(i, k):
                        if known(i) and i == 0 and k == 0:
                            exp_decay(0, 0)
                            exp_decay(0, 1)
                        copy_state(i, k - 1)
                        exp_decay(i, k + 2)
                        finish_groups(finish, i, k)

                    def finish(g, k):
                        if k == K_XN_FEAT:
                            after(act, "f_xn_t_ready", g)
                            nc.scalar.copy(xn_feat[:], ps[:, FA, 0:GTOK]).then_inc(G["f_xn_feat_ready"], 1)
                        if k in K_H1_RELU:
                            r = K_H1_RELU.index(k)
                            act.wait_ge(G["f_h1_proj"], g * 2 + r + 1)
                            nc.scalar.activation(h1[:, 2 * r:2 * r + 2, :].rearrange("p c t -> p (c t)"), ps[:, FB, :],
                                                 ACT.Relu, scale=s_col[:, 0:1]).then_inc(G["f_h1_ready"], 1)
                        if k == K_SQUARE:
                            after(act, "f_x1_ready", g)
                            after(act, "f_rrms_ready", g, back=1)
                            for j in range(GT):
                                m = nc.scalar.activation(square[:, j], x1[:, j], ACT.Square, accum_out=sumsq[:, j:j + 1])
                            m.then_inc(G["f_sumsq_ready"], 1)
                        if k == K_N2_FEAT:
                            after(act, "f_n2_t_ready", g)
                            nc.scalar.activation(n2_feat[:], ps[:, FA, 0:GTOK], ACT.Copy, scale=fw_col[:, 0:1]
                                                 ).then_inc(G["f_n2_feat_ready"], 1)
                        if k == K_GATE_TANH:
                            after(act, "f_gate_ready", g)
                            after(act, "f_silu_ready", g, back=1)
                            nc.scalar.activation(gate_tanh[:].rearrange("p h t -> p (h t)"), ps[:, FA, :], ACT.Tanh,
                                                 scale=0.5).then_inc(G["f_gate_tanh_ready"], 1)

                    chunks(act, step)
                    copy_state(BODIES - 1, STEPS - 1)
                    finish_last(finish)

                @block.vector
                def _(dve):
                    nc.vector.memset(state[:, RING - 1, 0:SELF], 0.0).then_inc(start_zeroed, 1)

                    def step(i, k):
                        t = i * STEPS + k
                        wait_step(dve, acc_decay_ready, t)
                        dve.wait_ge(acc_state, t + 1)
                        wait_step(dve, acc_copied, t - 2)
                        nc.vector.tensor_tensor(ps[:, ACCP + k % 2, :], decay[:, k % RING, SELF:QE],
                                                ps[:, ACCP + (k - 1) % 2, :], ALU.mult).then_inc(acc_decayed, 1)
                        wait_step(dve, self_input, t)
                        wait_step(dve, contracted, t - RING)
                        for p in range(Q // 2):
                            wait_step(dve, self_decayed[p], t)
                            nc.vector.tensor_tensor(state[:, k % RING, p * E:(p + 1) * E], decayed[:, p],
                                                    ps[:, SELFP, p * E:(p + 1) * E], ALU.add
                                                    ).then_inc(self_state[p], 1)
                        chunk = i * 2 + k // TC
                        if k % TC == LAG - 1 and not (known(t) and t < TC):
                            keep_y(chunk - 1, i + k // TC - 1, (k // TC + 1) % 2)
                        if k % TC == LAG + 5 and not (known(t) and t < TC or known(chunk) and chunk == NC - 1):
                            place_c(chunk + 1, (k // TC + 1) % 2)
                        finish_groups(finish, i, k)

                    def place_c(chunk, cb):
                        for bb in range(2):
                            m = nc.vector.tensor_copy(
                                c_cols[bb * N:(bb + 1) * N, cb, :, bb * TC:bb * TC + (TC - 1) * (2 * TC + 1) + 1:2 * TC + 1],
                                c_feat[bb * N:(bb + 1) * N, :, bass.ds(chunk * TC, TC)])
                        m.then_inc(c_placed, 1)

                    def keep_y(chunk, g, cb):
                        dve.wait_ge(contracted, (chunk + 1) * TC)
                        after(dve, "f_y_t_ready", g, back=1)
                        nc.vector.tensor_copy(y_tok[:, cb], ps[:, YP, 0:E]).then_inc(y_kept, 1)

                    def finish(g, k):
                        if k == K_STATS:
                            dve.wait_ge(G["f_x_loaded"], (g + 1) * (16 * GT))
                            after(dve, "f_rstd_ready", g, back=1)
                            for j in range(GT):
                                m = nc.vector.bn_stats(f_stats[:, j], x_in[:, j])
                            m.then_inc(G["f_stats_ready"], 1)
                            after(dve, "f_stats_ready", g)
                            nc.vector.memset(wait_mark[:], 0.0)
                            for j in range(GT):
                                m = nc.vector.bn_aggr(f_mv[:, j], f_stats[:, j])
                            m.then_inc(G["f_mv_ready"], 1)
                        if k == K_XN:
                            after(dve, "f_rstd_ready", g)
                            after(dve, "f_xn_t_ready", g, back=1)
                            for j in range(GT):
                                m = nc.vector.tensor_scalar(xn[:, j], x_in[:, j], f_mv[:, j, 0:1], f_nrm[:, 1, j:j + 1],
                                                            ALU.subtract, ALU.mult)
                            m.then_inc(G["f_xn_ready"], 1)
                        if k == K_GATED:
                            after(dve, "f_y_t_ready", g)
                            after(dve, "f_proj_ready", g, back=1)
                            for h in range(EH):
                                for j in range(GT):
                                    m = nc.vector.tensor_tensor(
                                        gated[:, h, j * P:(j + 1) * P].rearrange("e (b t) -> e b t", b=B),
                                        ps[:, FA, (h * GT + j) * P:(h * GT + j + 1) * P]
                                        .rearrange("e (b t) -> e b t", b=B),
                                        silu_z[:, h, :, bass.ds(g * TG + j * TC, TC)], ALU.mult)
                            m.then_inc(G["f_gated_ready"], 1)
                        if k == K_X1:
                            after(dve, "f_proj_ready", g)
                            after(dve, "f_base", g, back=1)
                            after(dve, "f_n2_ready", g, back=1)
                            nc.vector.tensor_tensor(x1[:].rearrange("p j d -> p (j d)"), ps[:, FA, 0:GT * D],
                                                    xn[:].rearrange("p j d -> p (j d)"), ALU.add
                                                    ).then_inc(G["f_x1_ready"], 1)
                        if k == K_N2:
                            after(dve, "f_rrms_ready", g)
                            after(dve, "f_n2_t_ready", g, back=1)
                            for j in range(GT):
                                m = nc.vector.tensor_scalar(n2[:, j], x1[:, j], f_nrm[:, 3, j:j + 1], None, ALU.mult)
                            m.then_inc(G["f_n2_ready"], 1)
                        if k == K_SILU:
                            after(dve, "f_gate_tanh_ready", g)
                            after(dve, "f_hid_ready", g, back=1)
                            nc.vector.scalar_tensor_tensor(gate_s[:].rearrange("p h t -> p (h t)"),
                                                           gate_tanh[:].rearrange("p h t -> p (h t)"), 1.0, ps[:, FA, :],
                                                           ALU.add, ALU.mult).then_inc(G["f_silu_ready"], 1)
                        if k == K_HID:
                            after(dve, "f_up_ready", g)
                            after(dve, "f_silu_ready", g)
                            after(dve, "f_sum_ready", g, back=1)
                            nc.vector.scalar_tensor_tensor(hid[:].rearrange("p h t -> p (h t)"),
                                                           gate_s[:].rearrange("p h t -> p (h t)"), 0.5, ps[:, FA, :],
                                                           ALU.mult, ALU.mult).then_inc(G["f_hid_ready"], 1)
                        if k in K_H2_RELU:
                            r = K_H2_RELU.index(k)
                            dve.wait_ge(G["f_h2_proj"], g * 2 + r + 1)
                            nc.vector.tensor_scalar(h2[:, 2 * r:2 * r + 2, :].rearrange("p c t -> p (c t)"), ps[:, FB, :],
                                                    s_fold[:, 0:1], 0.0, ALU.mult, ALU.max).then_inc(G["f_h2_ready"], 1)
                        if k == K_RESULT:
                            after(dve, "f_sum_ready", g)
                            after(dve, "f_base", g)
                            after(dve, "f_stored", g, per=16 * GT, back=1)
                            nc.vector.tensor_tensor(result[:].rearrange("p j d -> p (j d)"), ps[:, FB, 0:GT * D],
                                                    base[:].rearrange("p j d -> p (j d)"), ALU.add
                                                    ).then_inc(G["f_result"], 1)

                    place_c(0, 0)
                    place_c(1, 1)
                    chunks(dve, step)
                    keep_y(NC - 1, NG - 1, 1)
                    finish_last(finish)


_INS = ["L0_attn_x", "L0_attn_input_norm_w", "L0_attn_ffn_norm_w", "L0_attn_in_proj_W", "L0_attn_conv_W",
        "L0_attn_conv_b", "L0_attn_dt_W", "L0_attn_dt_b", "L0_attn_B_W", "L0_attn_C_W", "L0_attn_A_log",
        "L0_attn_out_proj_W", "L0_attn_gate_W", "L0_attn_up_W", "L0_attn_down_W", "L0_ffn_k0", "L0_ffn_k1",
        "L0_ffn_k2", "L0_ffn_s0", "L0_ffn_s1", "L0_ffn_s2"]


def kernel(**inputs):
    import numpy as _np
    import concourse.bacc as _bacc
    from concourse import mybir as _mybir
    from concourse.bass_utils import run_bass_kernel_spmd as _run

    nc = _bacc.Bacc("TRN2", target_bir_lowering=False, num_devices=1)
    arrays, args = {}, []
    for name in _INS:
        a = _np.ascontiguousarray(inputs[name])
        if a.ndim == 0:
            a = a.reshape(1)
        arrays[f"in_{name}_dram"] = a
        args.append(nc.dram_tensor(f"in_{name}_dram", a.shape, _mybir.dt.from_np(a.dtype), kind="ExternalInput").ap())
    shape = tuple(inputs["L0_attn_x"].shape)
    args.append(nc.dram_tensor("out_0_dram", shape, _mybir.dt.from_np(_np.dtype("float32")), kind="ExternalOutput").ap())
    mamba_and_binary_mlp_block(nc, *args)
    r = _run(nc, [arrays], core_ids=[0])
    return r.results[0]["out_0_dram"]
```

```python
from contextlib import ExitStack

import concourse.bass as bass
from concourse import mybir

F32 = mybir.dt.float32
BF16 = mybir.dt.bfloat16
U8 = mybir.dt.uint8
ALU = mybir.AluOpType
ACT = mybir.ActivationFunctionType

P = 128
EPS = 1e-5
DT_MIN, DT_MAX = 0.001, 0.1


def mamba_and_binary_mlp_block(nc: bass.Bass, x, norm_w, ffn_w, in_w, conv_w, conv_b, dt_w, dt_b, b_w, c_w,
                               a_log, out_w, gate_w, up_w, down_w, k0, k1, k2, s0, s1, s2, out):
    B, T, D = x.shape
    E = in_w.shape[1] // 2
    N = a_log.shape[0]
    I = gate_w.shape[1]
    H1, H2 = k0.shape[1], k1.shape[1]
    EH = E // P
    IH = I // P
    NJ = T // P
    NP = 3
    Q = B // 2
    TAPS = conv_w.shape[0]
    PAD_L = (TAPS - 1) // 2
    TPAD = T + TAPS - 1
    assert D == P and 2 * N == P and T % P == 0

    TC = 16
    NC = T // TC
    UROWS = NP * NP * B
    KROWS = UROWS + NP * B
    QE = Q * E
    SELF = QE // 2
    RING = 4
    STEPS = 2 * TC
    LAG = 2

    TG = STEPS
    NG = T // TG
    BODIES = T // STEPS
    GT = TG // TC
    GTOK = GT * P

    u_stage = nc.dram_tensor("u_stage", (NP, B, T, E), BF16, kind="Internal").ap()
    dt_stage = nc.dram_tensor("dt_stage", (NP, B, T, E), BF16, kind="Internal").ap()
    b_stage = nc.dram_tensor("b_stage", (NP, NP, B, T, N), BF16, kind="Internal").ap()

    with ExitStack() as ctx:
        def sb(name, shape, dt=F32):
            return ctx.enter_context(nc.sbuf_tensor(name, shape, dt))

        def sem(name):
            return ctx.enter_context(nc.semaphore(name))

        ps = ctx.enter_context(nc.psum_tensor("ps", [P, 8, 512], F32))

        ident = sb("ident", [P, P])
        zero_w = sb("zero_w", [P, P])
        mhalf = sb("mhalf", [P, NJ])
        w_in = sb("w_in", [P, 2 * E])
        w_tap = sb("w_tap", [P, TAPS, E])
        w_dtb = sb("w_dtb", [P, EH, E + N])
        w_c = sb("w_c", [P, EH, N])
        w_out = sb("w_out", [P, EH, D])
        w_gate = sb("w_gate", [P, I])
        w_up = sb("w_up", [P, I])
        w_down = sb("w_down", [P, IH, D])
        nw_col = sb("nw_col", [P, 1])
        fw_col = sb("fw_col", [P, 1])
        cb_col = sb("cb_col", [P, EH])
        dtb_bc = sb("dtb_bc", [P, E])
        a_col = sb("a_col", [P, 3])
        s_col = sb("s_col", [P, 3])
        s_fold = sb("s_fold", [P, 2])

        silu_z = sb("silu_z", [P, EH, B, T])
        c_feat = sb("c_feat", [P, Q, T])
        b_rows = sb("b_rows", [KROWS, 2, TC, Q, P], BF16)
        dt_pick = sb("dt_pick", [KROWS, Q, P], BF16)
        c_cols = sb("c_cols", [P, 2, Q, TC * 2 * TC])

        wait_mark = sb("wait_mark", [P, 1])
        inv_d = sb("inv_d", [P, NJ])
        eps_t = sb("eps_t", [P, NJ])
        first_weights = sem("first_weights")
        weights = sem("weights")
        const_zero = sem("const_zero")
        const_done = sem("const_done")
        taps_ready = sem("taps_ready")
        x_first_loaded = sem("x_first_loaded")
        x_rest_loaded = sem("x_rest_loaded")
        picks_zeroed = sem("picks_zeroed")
        picks_ready = sem("picks_ready")

        def settle(eng):
            eng.wait_ge(weights, NWEIGHTS)

        def wait_all(eng, waits):
            settle(eng)
            for s, v in waits:
                if not (isinstance(v, int) and v <= 0):
                    eng.wait_ge(s, v)

        c1 = ctx.enter_context(ExitStack())
        x_tok = c1.enter_context(nc.sbuf_tensor("x_tok", [P, B, NJ, D], F32))

        with ExitStack() as c0:
            conv_bc = c0.enter_context(nc.sbuf_tensor("conv_bc", [P, TAPS, E], F32))
            with nc.Block() as block:
                first_loads = [
                    (w_in[:], in_w),
                    (conv_bc[:], conv_w.rearrange("k o e -> o k e").partition_broadcast(P).rearrange("p o k e -> p (o k) e")),
                    (nw_col[:], norm_w.unsqueeze(1)),
                ] + [(cb_col[:, h:h + 1], conv_b[h * P:(h + 1) * P].unsqueeze(1)) for h in range(EH)]
                loads = [
                    (w_dtb[:, :, 0:E], dt_w.rearrange("(h p) e -> p h e", p=P)),
                    (w_dtb[:, :, E:E + N], b_w.rearrange("(h p) n -> p h n", p=P)),
                    (w_c[:], c_w.rearrange("(h p) n -> p h n", p=P)),
                    (dtb_bc[:], dt_b.partition_broadcast(P)),
                    (w_out[:], out_w.rearrange("(h p) d -> p h d", p=P)),
                    (w_gate[:], gate_w), (w_up[:], up_w), (w_down[:], down_w.rearrange("(h p) d -> p h d", p=P)),
                    (fw_col[:], ffn_w.unsqueeze(1)),
                    (a_col[0:N, 0:1], a_log.unsqueeze(1)), (a_col[N:P, 0:1], a_log.unsqueeze(1)),
                    (s_col[:, 0:1], s0.partition_broadcast(P)), (s_col[:, 1:2], s1.partition_broadcast(P)),
                    (s_col[:, 2:3], s2.partition_broadcast(P)),
                ]
                NFIRST = 16 * len(first_loads)
                NWEIGHTS = 16 * len(loads)

                tokens_in = x.rearrange("b (p j) d -> p b (j d)", j=NJ)
                x_rows = x_tok[:].rearrange("p b j d -> p b (j d)")

                @block.sync
                def _(sp):
                    sp.dma_start(x_rows[:, 0:2], tokens_in[:, 0:2]).then_inc(x_first_loaded, 16)
                    for dst, src in first_loads:
                        sp.dma_start(dst, src, allow_slow_non_contiguous=True).then_inc(first_weights, 16)

                @block.gpsimd
                def _(pool):
                    nc.gpsimd.memset(ident[:], 0.0).then_inc(const_zero, 1)
                    nc.gpsimd.memset(zero_w[:], 0.0)
                    nc.gpsimd.memset(mhalf[:], -0.5)
                    nc.gpsimd.memset(eps_t[:], EPS)
                    nc.gpsimd.memset(inv_d[:], 1.0 / D)
                    pool.wait_ge(const_zero, 1)
                    nc.gpsimd.affine_select(out=ident[:], in_=ident[:], compare_op=ALU.not_equal, fill=1.0, base=0,
                                            pattern=[[-1, P]], channel_multiplier=1).then_inc(const_done, 1)

                @block.vector
                def _(dve):
                    dve.wait_ge(first_weights, NFIRST)
                    for k in range(TAPS):
                        tap = nc.vector.tensor_tensor(w_tap[:, k, :], w_in[:, 0:E], conv_bc[:, k, :], ALU.mult)
                    tap.then_inc(taps_ready, 1)

        with c1:
            def pb(name, shape, dt=F32):
                return c1.enter_context(nc.sbuf_tensor(name, shape, dt))

            stats = pb("stats", [P, 2, NJ, 6])
            mean_var = pb("mean_var", [P, 2, NJ, 2])
            nrm = pb("nrm", [P, 6, NJ])
            normed = pb("normed", [P, 2, NJ, D])
            n_feat = pb("n_feat", [P, 2, TPAD])
            xc_feat = pb("xc_feat", [P, 2, EH, T])
            soft = pb("soft", [P, 3, NJ, E])
            dt_tok = pb("dt_tok", [P, NJ, E])
            u_tok = pb("u_tok", [P, NJ, E])
            dt_rest = pb("dt_rest", [P, NJ, E])
            u_rest = pb("u_rest", [P, NJ, E])
            b_tok = pb("b_tok", [P, NJ, N])
            b_rest = pb("b_rest", [P, NJ, N])
            dt_parts = pb("dt_parts", [P, 2, NP, NJ, E], BF16)
            u_parts = pb("u_parts", [P, 2, NP, NJ, E], BF16)
            b_parts = pb("b_parts", [P, 2, NP, NJ, N], BF16)

            names = ("stats_ready moments_ready rms_ready normed_ready normed_t_ready n_feat_ready "
                     "xc_proj_ready z_proj_ready xc_ready z_ready tok_proj_ready xc_t_ready b_proj_ready c_proj_ready c_ready "
                     "v_ready exp_ready p_ready ln_ready log_err_ready dt0_ready dt_ready u_ready "
                     "b_copied dt_split u_split b_split parts_stored0 parts_stored1 pads_ready nrm_step "
                     "dt_hi_ready u_hi_ready b_hi_ready dt_r1_ready u_r1_ready b_r1_ready dt_mid_ready u_mid_ready b_mid_ready w1_step")
            S = {n: sem(n) for n in names.split()}

            STORES = 4 + NP

            def batches(eng, slot, filling=None):
                def run(q, bb):
                    def at(stage, d):
                        sq, sbb = q + (bb + d) // 2, (bb + d) % 2
                        if not isinstance(q, int) or 0 <= sq * 2 + sbb < B:
                            stage(sq, sbb)
                    slot(at)

                for s in range(-1, 4):
                    run(s // 2, s % 2)
                    if s == 0 and filling is not None:
                        filling()
                with eng.Fori(2, Q - 1) as q:
                    for bb in range(2):
                        run(q, bb)
                for s in range(B - 2, B + 2):
                    run(s // 2, s % 2)

            def after(eng, name, n, per=1, back=0):
                if isinstance(n, int) and n - back < 0:
                    return
                eng.wait_ge(S[name], (n - back + 1) * per)

            NRM, BT, XC, DTT, CB, XCT = 0, 1, 2, 4, 6, 6

            with nc.Block() as block:
                @block.sync
                def _(sp):
                    for dst, src in loads:
                        sp.dma_start(dst, src, allow_slow_non_contiguous=True).then_inc(weights, 16)
                    sp.dma_start(x_rows[:, 2:B], tokens_in[:, 2:B]).then_inc(x_rest_loaded, 16)

                    def store(q, bb):
                        n = q * 2 + bb
                        for parts, stage, i0, i1, ready in (
                                [(dt_parts, dt_stage, 0, 2, "dt_mid_ready"), (u_parts, u_stage, 0, 2, "u_mid_ready"),
                                 (dt_parts, dt_stage, 2, 3, "dt_split"), (u_parts, u_stage, 2, 3, "u_split")]
                                + [(b_parts, b_stage[:, i], 0, NP, "b_split") for i in range(NP)]):
                            wait_all(sp, [(S[ready], n + 1)])
                            sp.dma_start(stage[i0:i1, bass.ds(n, 1)].rearrange("i o (p j) e -> (o p) i (j e)", j=NJ),
                                         parts[:, bb, i0:i1].rearrange("p i j e -> p i (j e)")
                                         ).then_inc(S[f"parts_stored{bb}"], 16)

                    for bb in range(2):
                        store(0, bb)
                    with sp.Fori(1, Q) as q:
                        for bb in range(2):
                            store(q, bb)
                    for bb in range(2):
                        sp.wait_ge(S[f"parts_stored{bb}"], Q * (16 * STORES))

                @block.gpsimd
                def _(pool):
                    nc.gpsimd.memset(n_feat[:, :, 0:PAD_L], 0.0)
                    nc.gpsimd.memset(n_feat[:, :, PAD_L + T:TPAD], 0.0).then_inc(S["pads_ready"], 1)

                    def norms(q, bb):
                        n = q * 2 + bb
                        after(pool, "moments_ready", n)
                        after(pool, "normed_ready", n, back=1)
                        var = mean_var[:, bb, :, 1]
                        steps = [
                            lambda: nc.gpsimd.tensor_tensor(nrm[:, 0], var, eps_t[:], ALU.add),
                            lambda: nc.gpsimd.tensor_tensor(nrm[:, 1], nrm[:, 0], mhalf[:], ALU.pow),
                            lambda: nc.gpsimd.tensor_tensor(nrm[:, 2], var, nrm[:, 1], ALU.mult),
                            lambda: nc.gpsimd.tensor_tensor(nrm[:, 3], nrm[:, 2], nrm[:, 1], ALU.mult),
                            lambda: nc.gpsimd.tensor_tensor(nrm[:, 3], nrm[:, 3], eps_t[:], ALU.add),
                            lambda: nc.gpsimd.tensor_tensor(nrm[:, 4], nrm[:, 3], mhalf[:], ALU.pow),
                        ]
                        for k, step in enumerate(steps):
                            step().then_inc(S["nrm_step"], 1)
                            pool.wait_ge(S["nrm_step"], n * len(steps) + k + 1)
                        nc.gpsimd.tensor_tensor(nrm[:, 5], nrm[:, 4], nrm[:, 1], ALU.mult).then_inc(S["rms_ready"], 1)

                    def log_err(q, bb):
                        n = q * 2 + bb
                        after(pool, "p_ready", n)
                        after(pool, "dt0_ready", n, back=1)
                        nc.gpsimd.tensor_tensor(soft[:, 2], soft[:, 2], soft[:, 1], ALU.subtract
                                                ).then_inc(S["log_err_ready"], 1)

                    def first_rest(q, bb):
                        n = q * 2 + bb
                        after(pool, "dt_hi_ready", n)
                        after(pool, "dt_split", n, back=1)
                        nc.gpsimd.tensor_tensor(dt_rest[:], dt_tok[:], dt_parts[:, bb, 0], ALU.subtract
                                                ).then_inc(S["dt_r1_ready"], 1)

                    def second_rest(q, bb):
                        n = q * 2 + bb
                        after(pool, "dt_mid_ready", n)
                        nc.gpsimd.tensor_tensor(dt_parts[:, bb, 2], dt_rest[:], dt_parts[:, bb, 1], ALU.subtract
                                                ).then_inc(S["dt_split"], 1)

                    def slot(at):
                        at(norms, 1)
                        at(first_rest, -2)
                        at(log_err, -1)
                        at(second_rest, -2)

                    def prepare_scan():
                        nc.gpsimd.memset(dt_pick[:], 0.0).then_inc(picks_zeroed, 1)
                        pool.wait_ge(picks_zeroed, 1)
                        for i in range(NP):
                            nc.gpsimd.affine_select(
                                out=dt_pick[:].rearrange("r q (b n) -> r q b n", b=2),
                                in_=dt_pick[:].rearrange("r q (b n) -> r q b n", b=2),
                                compare_op=ALU.not_equal, fill=1.0, base=-(UROWS + i * B),
                                pattern=[[-2, Q], [-1, 2], [0, N]], channel_multiplier=1).then_inc(picks_ready, 1)
                            pool.wait_ge(picks_ready, i + 1)
                        nc.gpsimd.memset(b_rows[:, 0], 0.0)

                    batches(pool, slot, prepare_scan)

                @block.tensor
                def _(pe):
                    pe.wait_ge(const_done, 1)
                    pe.wait_ge(taps_ready, 1)

                    def transpose_normed(q, bb):
                        n = q * 2 + bb
                        after(pe, "normed_ready", n)
                        after(pe, "z_ready", n, back=1)
                        for j in range(NJ):
                            m = nc.tensor.transpose(ps[:, NRM, j * P:(j + 1) * P], normed[:, bb, j], ident[:])
                        m.then_inc(S["normed_t_ready"], 1)

                    def project(q, bb):
                        n = q * 2 + bb
                        after(pe, "n_feat_ready", n)
                        after(pe, "xc_ready", n, back=1)
                        for h in range(EH):
                            for k in range(TAPS):
                                m = nc.tensor.matmul(ps[:, XC + h, :], w_tap[:, k, h * P:(h + 1) * P],
                                                     n_feat[:, bb, k:k + T], start=(k == 0), stop=(k == TAPS - 1))
                            m.then_inc(S["xc_proj_ready"], 1)
                        after(pe, "b_copied", n, back=1)
                        for h in range(EH):
                            m = nc.tensor.matmul(ps[:, NRM + h, :], w_in[:, E + h * P:E + (h + 1) * P],
                                                 n_feat[:, bb, PAD_L:PAD_L + T], start=True, stop=True)
                        m.then_inc(S["z_proj_ready"], 1)

                    def dt_products(q, bb):
                        n = q * 2 + bb
                        if isinstance(n, int) and n == 0:
                            pe.wait_ge(weights, NWEIGHTS)
                        after(pe, "xc_ready", n)
                        after(pe, "v_ready", n, back=1)
                        for j in range(NJ):
                            for h in range(EH):
                                m = nc.tensor.matmul(ps[:, DTT + j // 2, (j % 2) * E:(j % 2 + 1) * E],
                                                     xc_feat[:, bb, h, j:T:NJ], w_dtb[:, h, 0:E],
                                                     start=(h == 0), stop=(h == EH - 1))
                        m.then_inc(S["tok_proj_ready"], 1)

                    def bc_products(q, bb):
                        n = q * 2 + bb
                        after(pe, "u_ready", n, back=1)
                        for h in range(EH):
                            m = nc.tensor.matmul(ps[bb * N:(bb + 1) * N, CB, :], w_c[:, h, :], xc_feat[:, bb, h, :],
                                                 start=(h == 0), stop=(h == EH - 1))
                        m.then_inc(S["c_proj_ready"], 1)
                        after(pe, "z_ready", n)
                        for j in range(NJ):
                            for h in range(EH):
                                m = nc.tensor.matmul(ps[:, BT, j * N:(j + 1) * N],
                                                     xc_feat[:, bb, h, j:T:NJ], w_dtb[:, h, E:E + N],
                                                     start=(h == 0), stop=(h == EH - 1))
                        m.then_inc(S["b_proj_ready"], 1)
                        after(pe, "c_ready", n)
                        for j in range(NJ):
                            for h in range(EH):
                                m = nc.tensor.transpose(
                                    ps[:, XCT + j // 2, (j % 2) * E + h * P:(j % 2) * E + (h + 1) * P],
                                    xc_feat[:, bb, h, j:T:NJ], ident[:])
                        m.then_inc(S["xc_t_ready"], 1)

                    def slot(at):
                        at(dt_products, -1)
                        at(transpose_normed, 0)
                        at(bc_products, -1)
                        at(project, 0)

                    batches(pe, slot)

                @block.scalar
                def _(act):
                    act.wait_ge(first_weights, NFIRST)
                    act.wait_ge(S["pads_ready"], 1)

                    def normed_to_sbuf(q, bb):
                        n = q * 2 + bb
                        after(act, "normed_t_ready", n)
                        after(act, "z_proj_ready", n, back=2)
                        nc.scalar.activation(
                            n_feat[:, bb, PAD_L:PAD_L + T].rearrange("d (p j) -> d p j", j=NJ),
                            ps[:, NRM, :].rearrange("d (j p) -> d p j", j=NJ), ACT.Copy, scale=nw_col[:, 0:1]
                        ).then_inc(S["n_feat_ready"], 1)

                    def silus(q, bb):
                        n = q * 2 + bb
                        after(act, "xc_t_ready", n, back=2)
                        for h in range(EH):
                            act.wait_ge(S["xc_proj_ready"], n * EH + h + 1)
                            m = nc.scalar.activation(xc_feat[:, bb, h, :], ps[:, XC + h, :], ACT.Silu,
                                                     bias=cb_col[:, h:h + 1])
                        m.then_inc(S["xc_ready"], 1)
                        after(act, "z_proj_ready", n)
                        m = nc.scalar.activation(silu_z[:, :, bass.ds(n, 1), :].rearrange("p h o t -> p h (o t)"),
                                                 ps[:, NRM:NRM + EH, :], ACT.Silu)
                        m.then_inc(S["z_ready"], 1)

                    def c_to_sbuf(q, bb):
                        n = q * 2 + bb
                        after(act, "c_proj_ready", n)
                        nc.scalar.copy(c_feat[bb * N:(bb + 1) * N, bass.ds(q, 1), :].rearrange("p o t -> p (o t)"),
                                       ps[bb * N:(bb + 1) * N, CB, :]).then_inc(S["c_ready"], 1)

                    def dt_exp(q, bb):
                        n = q * 2 + bb
                        after(act, "v_ready", n)
                        nc.scalar.activation(soft[:, 0], soft[:, 0], ACT.Exp).then_inc(S["exp_ready"], 1)

                    def dt_log(q, bb):
                        n = q * 2 + bb
                        after(act, "p_ready", n)
                        nc.scalar.activation(soft[:, 0], soft[:, 1], ACT.Ln, bias=1.0).then_inc(S["ln_ready"], 1)

                    def first_parts(q, bb):
                        n = q * 2 + bb
                        if not (isinstance(q, int) and q == 0):
                            act.wait_ge(S[f"parts_stored{bb}"], q * (16 * STORES))
                        for kind, tok, parts, ready in (("dt", dt_tok, dt_parts, "dt_ready"),
                                                        ("u", u_tok, u_parts, "u_ready"),
                                                        ("b", b_tok, b_parts, "b_copied")):
                            after(act, ready, n)
                            nc.scalar.copy(parts[:, bb, 0], tok[:]).then_inc(S[kind + "_hi_ready"], 1)

                    def second_parts(q, bb):
                        n = q * 2 + bb
                        for kind, rest, parts in (("dt", dt_rest, dt_parts), ("u", u_rest, u_parts),
                                                  ("b", b_rest, b_parts)):
                            after(act, kind + "_r1_ready", n)
                            nc.scalar.copy(parts[:, bb, 1], rest[:]).then_inc(S[kind + "_mid_ready"], 1)

                    def slot(at):
                        at(first_parts, -2)
                        at(normed_to_sbuf, 0)
                        at(c_to_sbuf, -1)
                        at(dt_exp, -1)
                        at(second_parts, -2)
                        at(dt_log, -1)
                        at(silus, 0)

                    batches(act, slot)

                @block.vector
                def _(dve):
                    def moments(q, bb):
                        n = q * 2 + bb
                        if not isinstance(n, int) or n < 2:
                            dve.wait_ge(x_first_loaded, 16)
                        if not isinstance(n, int) or n >= 2:
                            dve.wait_ge(x_rest_loaded, 16)
                        for j in range(NJ):
                            m = nc.vector.bn_stats(stats[:, bb, j], token_tile(n, j))
                        m.then_inc(S["stats_ready"], 1)
                        after(dve, "stats_ready", n)
                        nc.vector.memset(wait_mark[:], 0.0)
                        for j in range(NJ):
                            m = nc.vector.bn_aggr(mean_var[:, bb, j], stats[:, bb, j])
                        m.then_inc(S["moments_ready"], 1)

                    def token_tile(n, j):
                        return x_tok[:, bass.ds(n, 1), j].rearrange("p o d -> p (o d)")

                    def normalize(q, bb):
                        n = q * 2 + bb
                        after(dve, "rms_ready", n)
                        after(dve, "normed_t_ready", n, back=2)
                        for j in range(NJ):
                            m = nc.vector.tensor_scalar(normed[:, bb, j], token_tile(n, j), mean_var[:, bb, j, 0:1],
                                                        nrm[:, 5, j:j + 1], ALU.subtract, ALU.mult)
                        m.then_inc(S["normed_ready"], 1)

                    def dt_bias(q, bb):
                        n = q * 2 + bb
                        after(dve, "tok_proj_ready", n)
                        if isinstance(n, int) and n == 0:
                            dve.wait_ge(weights, NWEIGHTS)
                        after(dve, "dt0_ready", n, back=1)
                        nc.vector.tensor_tensor(soft[:, 0],
                                                ps[:, DTT:DTT + 2, :].rearrange("p a (c e) -> p (a c) e", c=2),
                                                dtb_bc[:].unsqueeze(1).broadcast_to([P, NJ, E]), ALU.add
                                                ).then_inc(S["v_ready"], 1)

                    def b_to_sbuf(q, bb):
                        n = q * 2 + bb
                        after(dve, "b_proj_ready", n)
                        after(dve, "b_r1_ready", n, back=1)
                        nc.vector.tensor_copy(b_tok[:].rearrange("p j n -> p (j n)"), ps[:, BT, 0:NJ * N]
                                              ).then_inc(S["b_copied"], 1)

                    def exp_to_p(q, bb):
                        n = q * 2 + bb
                        after(dve, "exp_ready", n)
                        after(dve, "log_err_ready", n, back=1)
                        nc.vector.tensor_scalar(soft[:, 1], soft[:, 0], 1.0, None, ALU.min).then_inc(S["w1_step"], 1)
                        dve.wait_ge(S["w1_step"], n + 1)
                        nc.vector.tensor_scalar(soft[:, 2], soft[:, 1], 1.0, -1.0, ALU.add, ALU.add
                                                ).then_inc(S["p_ready"], 1)

                    def dt_and_u(q, bb):
                        n = q * 2 + bb
                        after(dve, "ln_ready", n)
                        after(dve, "log_err_ready", n)
                        nc.vector.tensor_tensor(soft[:, 0], soft[:, 0], soft[:, 2], ALU.subtract
                                                ).then_inc(S["dt0_ready"], 1)
                        after(dve, "dt0_ready", n)
                        after(dve, "dt_r1_ready", n, back=1)
                        nc.vector.tensor_scalar(dt_tok[:], soft[:, 0], DT_MIN, DT_MAX, ALU.max, ALU.min
                                                ).then_inc(S["dt_ready"], 1)
                        after(dve, "dt_ready", n)
                        after(dve, "xc_t_ready", n)
                        after(dve, "u_r1_ready", n, back=1)
                        nc.vector.tensor_tensor(u_tok[:].rearrange("p j e -> p (j e)"),
                                                ps[:, XCT:XCT + 2, :].rearrange("p a c -> p (a c)"),
                                                dt_tok[:].rearrange("p j e -> p (j e)"), ALU.mult
                                                ).then_inc(S["u_ready"], 1)

                    def first_rests(q, bb):
                        n = q * 2 + bb
                        after(dve, "u_hi_ready", n)
                        after(dve, "u_split", n, back=1)
                        nc.vector.tensor_tensor(u_rest[:], u_tok[:], u_parts[:, bb, 0], ALU.subtract
                                                ).then_inc(S["u_r1_ready"], 1)
                        after(dve, "b_hi_ready", n)
                        after(dve, "b_split", n, back=1)
                        nc.vector.tensor_tensor(b_rest[:], b_tok[:], b_parts[:, bb, 0], ALU.subtract
                                                ).then_inc(S["b_r1_ready"], 1)

                    def second_rests(q, bb):
                        n = q * 2 + bb
                        after(dve, "u_mid_ready", n)
                        nc.vector.tensor_tensor(u_parts[:, bb, 2], u_rest[:], u_parts[:, bb, 1], ALU.subtract
                                                ).then_inc(S["u_split"], 1)
                        after(dve, "b_mid_ready", n)
                        nc.vector.tensor_tensor(b_parts[:, bb, 2], b_rest[:], b_parts[:, bb, 1], ALU.subtract
                                                ).then_inc(S["b_split"], 1)

                    def slot(at):
                        at(moments, 1)
                        at(first_rests, -2)
                        at(dt_bias, -1)
                        at(normalize, 1)
                        at(b_to_sbuf, -1)
                        at(exp_to_p, -1)
                        at(second_rests, -2)
                        at(dt_and_u, -1)

                    def prepare_scan():
                        nc.vector.memset(c_cols[:], 0.0)
                        nc.vector.memset(b_rows[:, 1], 0.0)

                    batches(dve, slot, prepare_scan)

        with ExitStack() as c2:
            def pb(name, shape, dt=F32):
                return c2.enter_context(nc.sbuf_tensor(name, shape, dt))

            moving = pb("moving", [KROWS, 2, TC, E], BF16)
            decay = pb("decay", [P, RING, QE])
            state = pb("state", [P, RING, QE])
            decayed = pb("decayed", [P, Q // 2, E])

            k0_raw = pb("k0_raw", [P, 2, H1], U8)
            k1_raw = pb("k1_raw", [P, H1 // P, H2], U8)
            k2_raw = pb("k2_raw", [P, H2 // P, D], U8)
            k0_f = pb("k0_f", [P, H1])
            w0 = pb("w0", [P, H1])
            w1 = pb("w1", [P, H1 // P, H2])
            w2 = pb("w2", [P, H2 // P, D])
            bin_loaded = sem("bin_loaded")
            bin_step = sem("bin_step")
            bin_ready = sem("bin_ready")
            a_exp = sem("a_exp")
            a_ready = sem("a_ready")

            x_in = pb("x_in", [P, GT, D])
            y_tok = pb("y_tok", [P, GT, E])
            f_stats = pb("f_stats", [P, GT, 6])
            f_mv = pb("f_mv", [P, GT, 2])
            f_nrm = pb("f_nrm", [P, 4, GT])
            square = pb("square", [P, GT, D])
            sumsq = pb("sumsq", [P, GT])
            xn = pb("xn", [P, GT, D])
            xn_feat = pb("xn_feat", [P, GTOK])
            gated = pb("gated", [P, EH, GTOK])
            x1 = pb("x1", [P, GT, D])
            base = pb("base", [P, GT, D])
            n2 = pb("n2", [P, GT, D])
            n2_feat = pb("n2_feat", [P, GTOK])
            h1 = pb("h1", [P, H1 // P, GTOK])
            h2 = pb("h2", [P, H2 // P, GTOK])
            gate_tanh = pb("gate_tanh", [P, IH, GTOK])
            gate_s = pb("gate_s", [P, IH, GTOK])
            hid = pb("hid", [P, IH, GTOK])
            result = pb("result", [P, GT, D])
            names = ("f_x_loaded f_stats_ready f_mv_ready f_rstd_ready f_xn_ready f_xn_t_ready f_xn_feat_ready "
                     "f_y_t_ready f_gated_ready f_proj_ready f_x1_ready f_sumsq_ready f_rrms_ready f_n2_ready "
                     "f_n2_t_ready f_n2_feat_ready f_h1_proj f_h1_ready f_h2_proj f_h2_ready f_gate_ready "
                     "f_gate_tanh_ready f_silu_ready f_up_ready f_hid_ready f_sum_ready f_base "
                     "f_result f_stored f_rstd_sum f_mean_square f_rrms_sum")
            G = {n: sem(n) for n in names.split()}

            K_STATS, K_MOMENTS, K_RSTD_SUM, K_RSTD, K_XN, K_XN_T, K_XN_FEAT = -5, -4, -3, -2, -1, 2, 3
            K_Y_T, K_GATED, K_OUT, K_X1, K_SQUARE, K_RRMS_SUM, K_RRMS, K_BASE, K_N2 = 6, (7, 8), 9, 11, 12, 13, 15, 18, 17
            K_N2_T, K_N2_FEAT = 19, 20
            K_GATE, K_GATE_TANH, K_SILU, K_UP, K_HID = 22, 24, (25, 26), (30, 32), 33
            K_H1, K_H1_RELU = (7, 11), ((9, 10), (13,))
            K_H2, K_H2_RELU = (14, 24), ((22, 23), (32,))
            K_LAST, K_RESULT = 33, 38
            H2_STEPS, LAST_STEPS = 8, 5

            def finish_groups(finish, i, k):
                if not (isinstance(i, int) and i < 2):
                    finish(i - 2, STEPS + k)
                if not (isinstance(i, int) and i < 1):
                    finish(i - 1, k)
                if not (isinstance(i, int) and i >= NG):
                    finish(i, k - STEPS)

            def finish_last(finish):
                for k in range(STEPS):
                    finish_groups(finish, BODIES, k)
                for k in range(STEPS, K_RESULT + 1):
                    finish(NG - 1, k)

            def after(eng, name, g, per=1, back=0):
                if isinstance(g, int) and g - back < 0:
                    return
                eng.wait_ge(G[name], (g - back + 1) * per)

            def columns(ap, part, steps):
                n = ap.shape[-1] // len(steps)
                return ap[:, part * n:(part + 1) * n]

            def share(items, part, parts):
                return items[part * len(items) // parts:(part + 1) * len(items) // parts]

            chunk_loaded = [sem("chunk_loaded0"), sem("chunk_loaded1")]
            b_loaded = [sem("b_loaded0"), sem("b_loaded1")]
            start_zeroed = sem("start_zeroed")
            self_dt_spread = sem("self_dt_spread")
            acc_dt_spread = sem("acc_dt_spread")
            self_decay_ready = sem("self_decay_ready")
            acc_decay_ready = sem("acc_decay_ready")
            self_decayed = [sem(f"self_decayed{p}") for p in range(Q // 2)]
            acc_decayed = sem("acc_decayed")
            self_input = sem("self_input")
            acc_state = sem("acc_state")
            self_state = [sem(f"self_state{p}") for p in range(Q // 2)]
            acc_copied = sem("acc_copied")
            contracted = sem("contracted")
            y_kept = sem("y_kept")
            c_placed = sem("c_placed")

            DTP, SELFP, FA, ACCP, YP, FB = 0, 2, 3, 4, 6, 7
            LOADS = 2

            def chunks(eng, body):
                for i in range(3):
                    for k in range(STEPS):
                        body(i, k)
                with eng.Fori(3, BODIES - 1) as i:
                    for k in range(STEPS):
                        body(i, k)
                for k in range(STEPS):
                    body(BODIES - 1, k)

            def known(t):
                return isinstance(t, int)

            def wait_step(eng, s, t):
                if known(t) and t < 0:
                    return
                eng.wait_ge(s, t + 1)

            with nc.Block() as block:
                @block.sync
                def _(sp):
                    def load(t, cb):
                        sp.dma_start(moving[0:UROWS, cb].rearrange("r t e -> r (t e)"),
                                     u_stage[:, :, bass.ds(t, TC), :].rearrange("i b t e -> (i b) (t e)")
                                     .unsqueeze(0).broadcast_to([NP, NP * B, TC * E])
                                     ).then_inc(chunk_loaded[cb], 16)
                        sp.dma_start(moving[UROWS:KROWS, cb].rearrange("r t e -> r (t e)"),
                                     dt_stage[:, :, bass.ds(t, TC), :].rearrange("i b t e -> (i b) (t e)")
                                     ).then_inc(chunk_loaded[cb], 16)
                        for b in range(B):
                            q, bb = b // 2, b % 2
                            sp.dma_start(b_rows[b:UROWS:B, cb, :, q, bb * N:(bb + 1) * N],
                                         b_stage[:, :, b, bass.ds(t, TC), :].rearrange("j i t n -> (j i) t n")
                                         ).then_inc(b_loaded[cb], 16)

                    load(0, 0)
                    load(TC, 1)
                    for dst, src in ((k0_raw, k0), (k1_raw, k1), (k2_raw, k2)):
                        sp.dma_start(dst[:], src.rearrange("(h p) f -> p h f", p=P)).then_inc(bin_loaded, 16)
                    def load_tokens(g):
                        if not (known(g) and g == 0):
                            wait_all(sp, [(G["f_base"], g)])
                        for j in range(GT):
                            sp.dma_start(x_in[:, j, :], x[:, bass.ds(g * TG + j * TC, TC), :]
                                         ).then_inc(G["f_x_loaded"], 16)

                    def store(g):
                        wait_all(sp, [(G["f_result"], g + 1)])
                        for j in range(GT):
                            sp.dma_start(out[:, bass.ds(g * TG + j * TC, TC), :], result[:, j, :]
                                         ).then_inc(G["f_stored"], 16)

                    def body(i):
                        if not (known(i) and i < 3):
                            store(i - 3)
                        for cb in range(2):
                            wait_all(sp, [(acc_state, i * STEPS + (cb + 1) * TC - STEPS + 1)])
                            load(i * STEPS + cb * TC, cb)
                            if cb == 0:
                                load_tokens(i - 1)

                    body(1)
                    body(2)
                    with sp.Fori(3, BODIES) as i:
                        body(i)
                    store(NG - 3)
                    load_tokens(NG - 1)
                    store(NG - 2)
                    store(NG - 1)
                    sp.wait_ge(G["f_stored"], 16 * GT * NG)

                @block.gpsimd
                def _(pool):
                    def decay_self(i, k):
                        t = i * STEPS + k
                        wait_step(pool, self_decay_ready, t)
                        if known(t) and t == 0:
                            pool.wait_ge(start_zeroed, 1)
                        for p in range(Q // 2):
                            wait_step(pool, self_state[p], t - 1)
                            nc.gpsimd.tensor_tensor(decayed[:, p], decay[:, k % RING, p * E:(p + 1) * E],
                                                    state[:, (k - 1) % RING, p * E:(p + 1) * E], ALU.mult
                                                    ).then_inc(self_decayed[p], 1)

                    def finish(g, k):
                        if k == K_RSTD_SUM:
                            after(pool, "f_mv_ready", g)
                            after(pool, "f_xn_ready", g, back=1)
                            nc.gpsimd.tensor_tensor(f_nrm[:, 0], f_mv[:, :, 1], eps_t[:, 0:GT], ALU.add
                                                    ).then_inc(G["f_rstd_sum"], 1)
                        if k == K_RSTD:
                            after(pool, "f_rstd_sum", g)
                            nc.gpsimd.tensor_tensor(f_nrm[:, 1], f_nrm[:, 0], mhalf[:, 0:GT], ALU.pow
                                                    ).then_inc(G["f_rstd_ready"], 1)
                        if k == K_RRMS_SUM:
                            after(pool, "f_sumsq_ready", g)
                            after(pool, "f_n2_ready", g, back=1)
                            nc.gpsimd.tensor_tensor(f_nrm[:, 2], sumsq[:], inv_d[:, 0:GT], ALU.mult
                                                    ).then_inc(G["f_mean_square"], 1)
                            after(pool, "f_mean_square", g)
                            nc.gpsimd.tensor_tensor(f_nrm[:, 2], f_nrm[:, 2], eps_t[:, 0:GT], ALU.add
                                                    ).then_inc(G["f_rrms_sum"], 1)
                        if k == K_RRMS:
                            after(pool, "f_rrms_sum", g)
                            nc.gpsimd.tensor_tensor(f_nrm[:, 3], f_nrm[:, 2], mhalf[:, 0:GT], ALU.pow
                                                    ).then_inc(G["f_rrms_ready"], 1)
                        if k == K_BASE:
                            after(pool, "f_x1_ready", g)
                            after(pool, "f_result", g, back=1)
                            nc.gpsimd.tensor_tensor(base[:], x_in[:], x1[:], ALU.add).then_inc(G["f_base"], 1)

                    def step(i, k):
                        decay_self(i, k)
                        finish_groups(finish, i, k)

                    chunks(pool, step)
                    finish_last(finish)

                @block.tensor
                def _(pe):
                    for f in range(2):
                        for h in range(2):
                            m = nc.tensor.matmul(ps[:, ACCP + f, h * E:(h + 1) * E], zero_w[:, :], w_in[:, 0:E],
                                                 start=(h == 0), stop=(h == 1), skip_group_check=True)
                    m.then_inc(acc_state, 1)
                    pe.wait_ge(picks_ready, NP)

                    def spread_dt(i, k, pairs, ready, spread):
                        t = i * STEPS + k
                        if known(t) and t >= T:
                            return
                        cb, kk = (k // TC) % 2, k % TC
                        if kk == 0 and spread is self_dt_spread:
                            pe.wait_ge(chunk_loaded[cb], (i + k // STEPS + 1) * (16 * LOADS))
                        wait_step(pe, ready, t - 1)
                        for q in pairs:
                            m = nc.tensor.matmul(ps[:, DTP + q // 2, (q % 2) * E:(q % 2 + 1) * E], dt_pick[:, q, :],
                                                 moving[:, cb, kk, :], start=True, stop=True)
                        m.then_inc(spread, 1)

                    def spread_self(i, k):
                        spread_dt(i, k, range(Q // 2), self_decay_ready, self_dt_spread)

                    def spread_acc(i, k):
                        spread_dt(i, k, range(Q // 2, Q), acc_decay_ready, acc_dt_spread)

                    def contract(i, k):
                        t = i * STEPS + k
                        if known(t) and t < 0:
                            return
                        cb, kk = (k // TC) % 2, k % TC
                        if kk == 0:
                            chunk = i * 2 + k // TC
                            pe.wait_ge(c_placed, chunk + 1)
                            if not (known(chunk) and chunk < 1):
                                pe.wait_ge(y_kept, chunk)
                        wait_step(pe, self_state[1], t)
                        wait_step(pe, acc_copied, t)
                        for q in range(Q):
                            m = nc.tensor.matmul(ps[q * 32:(q + 1) * 32, YP, 0:E],
                                                 c_cols[:, cb, q, kk * 2 * TC:(kk + 1) * 2 * TC],
                                                 state[:, k % RING, q * E:(q + 1) * E],
                                                 start=(kk == 0), stop=(kk == TC - 1))
                        m.then_inc(contracted, 1)

                    def step(i, k):
                        t = i * STEPS + k
                        cb, kk = (k // TC) % 2, k % TC
                        if known(t) and t == 0:
                            for first in range(2):
                                spread_self(0, first)
                                spread_acc(0, first)
                            self_product(0, 0)
                        spread_self(i, k + 2)
                        wait_step(pe, acc_decayed, t)
                        for q in range(Q // 2, Q):
                            m = nc.tensor.matmul(ps[:, ACCP + k % 2, (q % 2) * E:(q % 2 + 1) * E],
                                                 b_rows[:, cb, kk, q, :], moving[:, cb, kk, :],
                                                 start=False, stop=False, skip_group_check=True)
                        m.then_inc(acc_state, 1)
                        spread_acc(i, k + 2)
                        if k % TC == LAG:
                            self_product(i, k + 1)
                            contract(i, k - LAG)
                        else:
                            contract(i, k - LAG)
                            self_product(i, k + 1)
                        finish_groups(finish, i, k)

                    def self_product(i, k):
                        t = i * STEPS + k
                        if known(t) and t >= T:
                            return
                        cb, kk = (k // TC) % 2, k % TC
                        if kk == 0:
                            pe.wait_ge(b_loaded[cb], (i + k // STEPS + 1) * (16 * B))
                        wait_step(pe, self_state[1], t - 1)
                        for q in range(Q // 2):
                            m = nc.tensor.matmul(ps[:, SELFP, q * E:(q + 1) * E], b_rows[:, cb, kk, q, :],
                                                 moving[:, cb, kk, :], start=True, stop=True)
                        m.then_inc(self_input, 1)

                    def finish(g, k):
                        if k == K_XN_T:
                            after(pe, "f_xn_ready", g)
                            after(pe, "f_hid_ready", g, back=1)
                            for j in range(GT):
                                m = nc.tensor.transpose(ps[:, FA, j * P:(j + 1) * P], xn[:, j], ident[:])
                            m.then_inc(G["f_xn_t_ready"], 1)
                        if k == K_Y_T:
                            pe.wait_ge(y_kept, (g + 1) * GT)
                            after(pe, "f_xn_feat_ready", g)
                            for h in range(EH):
                                for j in range(GT):
                                    m = nc.tensor.transpose(ps[:, FA, (h * GT + j) * P:(h * GT + j + 1) * P],
                                                            y_tok[:, j, h * P:(h + 1) * P], ident[:])
                            m.then_inc(G["f_y_t_ready"], 1)
                        j = k - K_OUT
                        if 0 <= j < GT:
                            if j == 0:
                                after(pe, "f_gated_ready", g)
                            for h in range(EH):
                                m = nc.tensor.matmul(ps[:, FA, j * P:(j + 1) * P], gated[:, h, j * P:(j + 1) * P],
                                                     w_out[:, h, :], start=(h == 0), stop=(h == EH - 1))
                            if j == GT - 1:
                                m.then_inc(G["f_proj_ready"], 1)
                        for r in range(2):
                            c = k - K_H1[r]
                            if 0 <= c < 2:
                                if c == 0 and r == 0 and known(g) and g == 0:
                                    pe.wait_ge(bin_ready, 3)
                                if c == 0 and r == 0:
                                    after(pe, "f_xn_feat_ready", g)
                                    after(pe, "f_result", g, back=1)
                                elif c == 0:
                                    pe.wait_ge(G["f_h1_ready"], g * 2 + r)
                                f = (2 * r + c) * P
                                m = nc.tensor.matmul(ps[:, FB, c * GTOK:(c + 1) * GTOK], w0[:, f:f + P], xn_feat[:],
                                                     start=True, stop=True)
                                if c == 1:
                                    m.then_inc(G["f_h1_proj"], 1)
                        if k == K_N2_T:
                            after(pe, "f_n2_ready", g)
                            for j in range(GT):
                                m = nc.tensor.transpose(ps[:, FA, j * P:(j + 1) * P], n2[:, j], ident[:])
                            m.then_inc(G["f_n2_t_ready"], 1)
                        h = k - K_GATE
                        if 0 <= h < IH:
                            if h == 0:
                                after(pe, "f_n2_feat_ready", g)
                            m = nc.tensor.matmul(ps[:, FA, h * GTOK:(h + 1) * GTOK], w_gate[:, h * P:(h + 1) * P],
                                                 n2_feat[:], start=True, stop=True)
                            if h == IH - 1:
                                m.then_inc(G["f_gate_ready"], 1)
                        if k in K_UP:
                            h = K_UP.index(k)
                            if h == 0:
                                after(pe, "f_silu_ready", g)
                            m = nc.tensor.matmul(ps[:, FA, h * GTOK:(h + 1) * GTOK], w_up[:, h * P:(h + 1) * P],
                                                 n2_feat[:], start=True, stop=True)
                            if h == IH - 1:
                                m.then_inc(G["f_up_ready"], 1)
                        for r in range(2):
                            part = k - K_H2[r]
                            if 0 <= part < H2_STEPS:
                                if part == 0 and r == 0:
                                    after(pe, "f_h1_ready", g, per=2)
                                elif part == 0:
                                    pe.wait_ge(G["f_h2_ready"], g * 2 + r)
                                for c, n in share([(c, n) for c in range(2) for n in range(H1 // P)], part, H2_STEPS):
                                    f = (2 * r + c) * P
                                    m = nc.tensor.matmul(ps[:, FB, c * GTOK:(c + 1) * GTOK], w1[:, n, f:f + P],
                                                         h1[:, n, :], start=(n == 0), stop=(n == H1 // P - 1))
                                if part == H2_STEPS - 1:
                                    m.then_inc(G["f_h2_proj"], 1)
                        part = k - K_LAST
                        if 0 <= part < LAST_STEPS:
                            if part == 0:
                                after(pe, "f_h2_ready", g, per=2)
                            if part == 1:
                                after(pe, "f_hid_ready", g)
                            terms = ([(h2[:, c], w2[:, c, :]) for c in range(H2 // P)]
                                     + [(hid[:, h], w_down[:, h, :]) for h in range(IH)])
                            for j, c in share([(j, c) for j in range(GT) for c in range(len(terms))], part, LAST_STEPS):
                                m = nc.tensor.matmul(ps[:, FB, j * P:(j + 1) * P], terms[c][0][:, j * P:(j + 1) * P],
                                                     terms[c][1], start=(c == 0), stop=(c == len(terms) - 1))
                            if part == LAST_STEPS - 1:
                                m.then_inc(G["f_sum_ready"], 1)

                    chunks(pe, step)
                    for k in range(LAG):
                        contract(BODIES - 1, STEPS - LAG + k)
                    finish_last(finish)

                @block.scalar
                def _(act):
                    act.wait_ge(weights, NWEIGHTS)
                    nc.scalar.activation(a_col[:, 1:2], a_col[:, 0:1], ACT.Exp).then_inc(a_exp, 1)
                    act.wait_ge(a_exp, 1)
                    nc.scalar.mul(a_col[:, 2:3], a_col[:, 1:2], -1.0).then_inc(a_ready, 1)
                    act.wait_ge(a_ready, 1)

                    def exp_decay(i, k):
                        t = i * STEPS + k
                        if known(t) and t >= T:
                            return
                        for f, spread, ready, used in ((0, self_dt_spread, self_decay_ready, self_decayed[1]),
                                                       (1, acc_dt_spread, acc_decay_ready, acc_decayed)):
                            wait_step(act, spread, t)
                            wait_step(act, used, t - RING)
                            nc.scalar.activation(decay[:, k % RING, f * SELF:(f + 1) * SELF], ps[:, DTP + f, :],
                                                 ACT.Exp, scale=a_col[:, 2:3]).then_inc(ready, 1)

                    def copy_state(i, k):
                        t = i * STEPS + k
                        if known(t) and t < 0:
                            return
                        act.wait_ge(acc_state, t + 2)
                        if not (known(t) and t == T - 1):
                            wait_step(act, acc_decayed, t + 1)
                        wait_step(act, contracted, t - RING)
                        nc.scalar.copy(state[:, k % RING, SELF:QE], ps[:, ACCP + k % 2, :]).then_inc(acc_copied, 1)

                    def step(i, k):
                        if known(i) and i == 0 and k == 0:
                            exp_decay(0, 0)
                            exp_decay(0, 1)
                        copy_state(i, k - 1)
                        exp_decay(i, k + 2)
                        finish_groups(finish, i, k)

                    def finish(g, k):
                        if k == K_SQUARE:
                            after(act, "f_x1_ready", g)
                            after(act, "f_rrms_ready", g, back=1)
                            for j in range(GT):
                                m = nc.scalar.activation(square[:, j], x1[:, j], ACT.Square, accum_out=sumsq[:, j:j + 1])
                            m.then_inc(G["f_sumsq_ready"], 1)
                        if k == K_GATE_TANH:
                            after(act, "f_gate_ready", g)
                            after(act, "f_silu_ready", g, back=1)
                            nc.scalar.activation(gate_tanh[:].rearrange("p h t -> p (h t)"), ps[:, FA, :], ACT.Tanh,
                                                 scale=0.5).then_inc(G["f_gate_tanh_ready"], 1)

                    chunks(act, step)
                    copy_state(BODIES - 1, STEPS - 1)
                    finish_last(finish)

                @block.vector
                def _(dve):
                    nc.vector.memset(state[:, RING - 1, 0:SELF], 0.0).then_inc(start_zeroed, 1)

                    def step(i, k):
                        t = i * STEPS + k
                        wait_step(dve, acc_decay_ready, t)
                        dve.wait_ge(acc_state, t + 1)
                        wait_step(dve, acc_copied, t - 2)
                        nc.vector.tensor_tensor(ps[:, ACCP + k % 2, :], decay[:, k % RING, SELF:QE],
                                                ps[:, ACCP + (k - 1) % 2, :], ALU.mult).then_inc(acc_decayed, 1)
                        chunk = i * 2 + k // TC
                        if k % TC == LAG and not (known(t) and t < TC):
                            keep_y(chunk - 1, i + k // TC - 1, (k // TC + 1) % 2)
                        wait_step(dve, self_input, t)
                        wait_step(dve, contracted, t - RING)
                        for p in range(Q // 2):
                            wait_step(dve, self_decayed[p], t)
                            nc.vector.tensor_tensor(state[:, k % RING, p * E:(p + 1) * E], decayed[:, p],
                                                    ps[:, SELFP, p * E:(p + 1) * E], ALU.add
                                                    ).then_inc(self_state[p], 1)
                        if k % TC == LAG + 8 and not (known(t) and t < TC or known(chunk) and chunk == NC - 1):
                            place_c(chunk + 1, (k // TC + 1) % 2)
                        if known(i) and i == 0:
                            binary_weights(k)
                        finish_groups(finish, i, k)

                    def binary_weights(k):
                        if k == 8:
                            dve.wait_ge(bin_loaded, 16 * 3)
                            nc.vector.tensor_copy(k0_f[:], k0_raw[:, 1, :]).then_inc(bin_step, 1)
                        if k == 10:
                            dve.wait_ge(weights, NWEIGHTS)
                            nc.vector.tensor_scalar(s_fold[:], s_col[:, 1:3], 2.0, None, ALU.mult).then_inc(bin_step, 1)
                        if k == 12:
                            dve.wait_ge(bin_step, 2)
                            nc.vector.tensor_tensor(w0[:], k0_raw[:, 0, :], k0_f[:], ALU.subtract).then_inc(bin_step, 1)
                        if k == 14:
                            nc.vector.tensor_scalar(w2[:], k2_raw[:], 2.0, -1.0, ALU.mult, ALU.add).then_inc(bin_step, 1)
                        if k == 16:
                            dve.wait_ge(bin_step, 4)
                            nc.vector.tensor_scalar(w0[:], w0[:], 2.0, None, ALU.mult).then_inc(bin_ready, 1)
                        if k == 18:
                            nc.vector.tensor_scalar(w2[:], w2[:], s_fold[:, 1:2], None, ALU.mult).then_inc(bin_ready, 1)
                        if k == 20:
                            nc.vector.tensor_scalar(w1[:], k1_raw[:], 2.0, -1.0, ALU.mult, ALU.add).then_inc(bin_ready, 1)

                    def place_c(chunk, cb):
                        for bb in range(2):
                            m = nc.vector.tensor_copy(
                                c_cols[bb * N:(bb + 1) * N, cb, :, bb * TC:bb * TC + (TC - 1) * (2 * TC + 1) + 1:2 * TC + 1],
                                c_feat[bb * N:(bb + 1) * N, :, bass.ds(chunk * TC, TC)])
                        m.then_inc(c_placed, 1)

                    def keep_y(chunk, g, cb):
                        dve.wait_ge(contracted, (chunk + 1) * TC)
                        after(dve, "f_y_t_ready", g, back=1)
                        nc.vector.tensor_copy(y_tok[:, cb], ps[:, YP, 0:E]).then_inc(y_kept, 1)

                    def finish(g, k):
                        if k == K_STATS:
                            dve.wait_ge(G["f_x_loaded"], (g + 1) * (16 * GT))
                            after(dve, "f_rstd_ready", g, back=1)
                            for j in range(GT):
                                m = nc.vector.bn_stats(f_stats[:, j], x_in[:, j])
                            m.then_inc(G["f_stats_ready"], 1)
                        if k == K_MOMENTS:
                            after(dve, "f_stats_ready", g)
                            nc.vector.memset(wait_mark[:], 0.0)
                            for j in range(GT):
                                m = nc.vector.bn_aggr(f_mv[:, j], f_stats[:, j])
                            m.then_inc(G["f_mv_ready"], 1)
                        if k == K_XN:
                            after(dve, "f_rstd_ready", g)
                            after(dve, "f_xn_t_ready", g, back=1)
                            for j in range(GT):
                                m = nc.vector.tensor_scalar(xn[:, j], x_in[:, j], f_mv[:, j, 0:1], f_nrm[:, 1, j:j + 1],
                                                            ALU.subtract, ALU.mult)
                            m.then_inc(G["f_xn_ready"], 1)
                        if k == K_XN_FEAT:
                            after(dve, "f_xn_t_ready", g)
                            nc.vector.tensor_copy(xn_feat[:], ps[:, FA, 0:GTOK]).then_inc(G["f_xn_feat_ready"], 1)
                        if k == K_N2_FEAT:
                            after(dve, "f_n2_t_ready", g)
                            nc.vector.tensor_scalar(n2_feat[:], ps[:, FA, 0:GTOK], fw_col[:, 0:1], None, ALU.mult
                                                    ).then_inc(G["f_n2_feat_ready"], 1)
                        if k in K_GATED:
                            h = K_GATED.index(k)
                            if h == 0:
                                after(dve, "f_y_t_ready", g)
                                after(dve, "f_proj_ready", g, back=1)
                            for j in range(GT):
                                m = nc.vector.tensor_tensor(
                                    gated[:, h, j * P:(j + 1) * P].rearrange("e (b t) -> e b t", b=B),
                                    ps[:, FA, (h * GT + j) * P:(h * GT + j + 1) * P]
                                    .rearrange("e (b t) -> e b t", b=B),
                                    silu_z[:, h, :, bass.ds(g * TG + j * TC, TC)], ALU.mult)
                            if h == EH - 1:
                                m.then_inc(G["f_gated_ready"], 1)
                        if k == K_X1:
                            after(dve, "f_proj_ready", g)
                            after(dve, "f_base", g, back=1)
                            after(dve, "f_n2_ready", g, back=1)
                            nc.vector.tensor_tensor(x1[:].rearrange("p j d -> p (j d)"), ps[:, FA, 0:GT * D],
                                                    xn[:].rearrange("p j d -> p (j d)"), ALU.add
                                                    ).then_inc(G["f_x1_ready"], 1)
                        if k == K_N2:
                            after(dve, "f_rrms_ready", g)
                            after(dve, "f_n2_t_ready", g, back=1)
                            for j in range(GT):
                                m = nc.vector.tensor_scalar(n2[:, j], x1[:, j], f_nrm[:, 3, j:j + 1], None, ALU.mult)
                            m.then_inc(G["f_n2_ready"], 1)
                        if k in K_SILU:
                            part = K_SILU.index(k)
                            if part == 0:
                                after(dve, "f_gate_tanh_ready", g)
                                after(dve, "f_hid_ready", g, back=1)
                            m = nc.vector.scalar_tensor_tensor(
                                columns(gate_s[:].rearrange("p h t -> p (h t)"), part, K_SILU),
                                columns(gate_tanh[:].rearrange("p h t -> p (h t)"), part, K_SILU), 1.0,
                                columns(ps[:, FA, :], part, K_SILU), ALU.add, ALU.mult)
                            if k == K_SILU[-1]:
                                m.then_inc(G["f_silu_ready"], 1)
                        if k == K_HID:
                            after(dve, "f_up_ready", g)
                            after(dve, "f_silu_ready", g)
                            after(dve, "f_sum_ready", g, back=1)
                            nc.vector.scalar_tensor_tensor(hid[:].rearrange("p h t -> p (h t)"),
                                                           gate_s[:].rearrange("p h t -> p (h t)"), 0.5, ps[:, FA, :],
                                                           ALU.mult, ALU.mult).then_inc(G["f_hid_ready"], 1)
                        for r in range(2):
                            if k in K_H1_RELU[r]:
                                part = K_H1_RELU[r].index(k)
                                if part == 0:
                                    dve.wait_ge(G["f_h1_proj"], g * 2 + r + 1)
                                m = nc.vector.tensor_scalar(
                                    columns(h1[:, 2 * r:2 * r + 2, :].rearrange("p c t -> p (c t)"), part, K_H1_RELU[r]),
                                    columns(ps[:, FB, :], part, K_H1_RELU[r]), s_col[:, 0:1], 0.0, ALU.mult, ALU.max)
                                if k == K_H1_RELU[r][-1]:
                                    m.then_inc(G["f_h1_ready"], 1)
                            if k in K_H2_RELU[r]:
                                part = K_H2_RELU[r].index(k)
                                if part == 0:
                                    dve.wait_ge(G["f_h2_proj"], g * 2 + r + 1)
                                m = nc.vector.tensor_scalar(
                                    columns(h2[:, 2 * r:2 * r + 2, :].rearrange("p c t -> p (c t)"), part, K_H2_RELU[r]),
                                    columns(ps[:, FB, :], part, K_H2_RELU[r]), s_fold[:, 0:1], 0.0, ALU.mult, ALU.max)
                                if k == K_H2_RELU[r][-1]:
                                    m.then_inc(G["f_h2_ready"], 1)
                        if k == K_RESULT:
                            after(dve, "f_sum_ready", g)
                            after(dve, "f_base", g)
                            after(dve, "f_stored", g, per=16 * GT, back=1)
                            nc.vector.tensor_tensor(result[:].rearrange("p j d -> p (j d)"), ps[:, FB, 0:GT * D],
                                                    base[:].rearrange("p j d -> p (j d)"), ALU.add
                                                    ).then_inc(G["f_result"], 1)

                    place_c(0, 0)
                    place_c(1, 1)
                    chunks(dve, step)
                    keep_y(NC - 1, NG - 1, 1)
                    finish_last(finish)


_INS = ["L0_attn_x", "L0_attn_input_norm_w", "L0_attn_ffn_norm_w", "L0_attn_in_proj_W", "L0_attn_conv_W",
        "L0_attn_conv_b", "L0_attn_dt_W", "L0_attn_dt_b", "L0_attn_B_W", "L0_attn_C_W", "L0_attn_A_log",
        "L0_attn_out_proj_W", "L0_attn_gate_W", "L0_attn_up_W", "L0_attn_down_W", "L0_ffn_k0", "L0_ffn_k1",
        "L0_ffn_k2", "L0_ffn_s0", "L0_ffn_s1", "L0_ffn_s2"]


def kernel(**inputs):
    import numpy as _np
    import concourse.bacc as _bacc
    from concourse import mybir as _mybir
    from concourse.bass_utils import run_bass_kernel_spmd as _run

    nc = _bacc.Bacc("TRN2", target_bir_lowering=False, num_devices=1)
    arrays, args = {}, []
    for name in _INS:
        a = _np.ascontiguousarray(inputs[name])
        if a.ndim == 0:
            a = a.reshape(1)
        arrays[f"in_{name}_dram"] = a
        args.append(nc.dram_tensor(f"in_{name}_dram", a.shape, _mybir.dt.from_np(a.dtype), kind="ExternalInput").ap())
    shape = tuple(inputs["L0_attn_x"].shape)
    args.append(nc.dram_tensor("out_0_dram", shape, _mybir.dt.from_np(_np.dtype("float32")), kind="ExternalOutput").ap())
    mamba_and_binary_mlp_block(nc, *args)
    r = _run(nc, [arrays], core_ids=[0])
    return r.results[0]["out_0_dram"]
```
